# Optimizing a Trainium2 kernel written in Bass

```python
import numpy as np
import jax
import jax.numpy as jnp

def _softmax(x, axis=-1):
    return jax.nn.softmax(x, axis=axis)

def _gelu(x):
    return jax.nn.gelu(x, approximate=True)

def _silu(x):
    return jax.nn.silu(x)

def _sigmoid(x):
    return jax.nn.sigmoid(x)

def _layernorm(x, axis=-1, eps=1e-05):
    m = jnp.mean(x, axis=axis, keepdims=True)
    v = jnp.var(x, axis=axis, keepdims=True)
    return (x - m) / jnp.sqrt(v + eps)

def _scatter_add(tgt, idx, src, axis=0):
    return tgt.at[idx].add(src)

def _segment_sum(src, seg, n):
    return jax.ops.segment_sum(src, seg, n)
kernel_name = 'mk_conv_attn_hybrid_d2_conv_nhwc128_r4_d35eea'

def setup_inputs(seed: int=0):
    np.random.seed(seed)
    _w = jnp.asarray

    def _rec_inputs():
        import jax
        import jax.numpy as jnp
        _gk = jax.random.key(seed)
        x = 0.0001032 + 1 * jax.random.normal(jax.random.fold_in(_gk, 1), (16, 32, 32, 32), jnp.float32)
        return x
    x = _rec_inputs()

    def _L0_conv_setup():
        import jax, jax.numpy as jnp
        import numpy as np
        IN_SIZE = 32
        OUT_SIZE = 32
        FILTER_SIZE = 6
        UP_FACTOR = 2
        DN_FACTOR = 2
        SLOPE = 0.2
        GAIN = float(np.sqrt(2.0))

        def _firwin_kaiser(numtaps, cutoff, width, fs):
            nyq = 0.5 * fs
            atten = 2.285 * (numtaps - 1) * np.pi * (width / nyq) + 7.95
            if atten > 50:
                beta = 0.1102 * (atten - 8.7)
            elif atten > 21:
                beta = 0.5842 * (atten - 21) ** 0.4 + 0.07886 * (atten - 21)
            else:
                beta = 0.0
            c = cutoff / nyq
            alpha = 0.5 * (numtaps - 1)
            m = np.arange(numtaps) - alpha
            h = c * np.sinc(c * m)
            h *= np.kaiser(numtaps, beta)
            h /= h.sum()
            return h.astype(np.float32)

        def _make_filter(size, factor):
            taps = FILTER_SIZE * factor
            f1d = _firwin_kaiser(taps, size / 2.0001, size, size)
            f2d = np.outer(f1d, f1d)[None, None]
            return jnp.asarray(f2d, dtype=jnp.float32)

        def _conv_same(x, f):
            k = f.shape[-1]
            pl = (k - 1) // 2
            pr = k - 1 - pl
            return jax.lax.conv_general_dilated(x, f, (1, 1), [(pl, pr), (pl, pr)])
        key = jax.random.key(seed)
        x = jax.random.normal(key, (16, 32, IN_SIZE, IN_SIZE), dtype=jnp.float32)
        bias = jnp.zeros((1, 32, 1, 1), dtype=jnp.float32)
        up_filter = _make_filter(IN_SIZE, UP_FACTOR)
        dn_filter = _make_filter(OUT_SIZE, DN_FACTOR)
        return {'x': x, 'bias': bias, 'up_filter': up_filter, 'dn_filter': dn_filter}
    _L0_conv_all = _L0_conv_setup()
    _L0_conv_in = {k: v for k, v in _L0_conv_all.items() if k in ('bias', 'up_filter', 'dn_filter')}
    del _L0_conv_all

    def _L1_attn_setup():
        import jax, jax.numpy as jnp
        import numpy as np
        B, S, D = (4, 1024, 32)
        key = jax.random.key(seed)
        kx, kq, kk, kv = jax.random.split(key, 4)
        x = jax.random.normal(kx, (B, S, D), dtype=jnp.float32)
        Wq = jax.random.normal(kq, (D, D), dtype=jnp.float32) * (1.0 / np.sqrt(D))
        Wk = jax.random.normal(kk, (D, D), dtype=jnp.float32) * (1.0 / np.sqrt(D))
        Wv = jax.random.normal(kv, (D, D), dtype=jnp.float32) * (1.0 / np.sqrt(D))
        return {'x': x, 'Wq': Wq, 'Wk': Wk, 'Wv': Wv}
    _L1_attn_all = _L1_attn_setup()
    _L1_attn_in = {k: v for k, v in _L1_attn_all.items() if k in ('Wq', 'Wk', 'Wv')}
    del _L1_attn_all

    def _L1_ffn_setup():
        import jax, jax.numpy as jnp
        import numpy as np
        B, S, D, E, H, O, K = (128, 512, 32, 16, 128, 32, 8)
        key = jax.random.key(seed)
        k0, k1, k2, k3 = jax.random.split(key, 4)
        x = jax.random.normal(k0, (B, S, D), dtype=jnp.float32)
        gate_w = jax.random.normal(k1, (E, D), dtype=jnp.float32) * (1.0 / np.sqrt(D))
        gate_b = jnp.zeros((E,), dtype=jnp.float32)
        weight1 = jax.random.uniform(k2, (E, D + 1, H), dtype=jnp.float32, minval=-1.0, maxval=1.0) * (1.0 / np.sqrt(D + 1))
        weight2 = jax.random.uniform(k3, (E, H + 1, O), dtype=jnp.float32, minval=-1.0, maxval=1.0) * (1.0 / np.sqrt(H + 1))
        return {'x': x, 'gate_w': gate_w, 'gate_b': gate_b, 'weight1': weight1, 'weight2': weight2}
    _L1_ffn_all = _L1_ffn_setup()
    _L1_ffn_in = {k: v for k, v in _L1_ffn_all.items() if k in ('gate_w', 'gate_b', 'weight1', 'weight2')}
    del _L1_ffn_all
    return {'x': x, 'L0_conv_bias': _L0_conv_in['bias'], 'L0_conv_up_filter': _L0_conv_in['up_filter'], 'L0_conv_dn_filter': _L0_conv_in['dn_filter'], 'L1_attn_Wq': _L1_attn_in['Wq'], 'L1_attn_Wk': _L1_attn_in['Wk'], 'L1_attn_Wv': _L1_attn_in['Wv'], 'L1_ffn_gate_w': _L1_ffn_in['gate_w'], 'L1_ffn_gate_b': _L1_ffn_in['gate_b'], 'L1_ffn_weight1': _L1_ffn_in['weight1'], 'L1_ffn_weight2': _L1_ffn_in['weight2']}

def reference(x, L0_conv_bias, L0_conv_up_filter, L0_conv_dn_filter, L1_attn_Wq, L1_attn_Wk, L1_attn_Wv, L1_ffn_gate_w, L1_ffn_gate_b, L1_ffn_weight1, L1_ffn_weight2):
    import jax
    import jax.numpy as jnp

    def _L0_conv_ref(x, bias, up_filter, dn_filter):
        import jax, jax.numpy as jnp
        import numpy as np
        IN_SIZE = 32
        OUT_SIZE = 32
        FILTER_SIZE = 6
        UP_FACTOR = 2
        DN_FACTOR = 2
        SLOPE = 0.2
        GAIN = float(np.sqrt(2.0))

        def _firwin_kaiser(numtaps, cutoff, width, fs):
            nyq = 0.5 * fs
            atten = 2.285 * (numtaps - 1) * np.pi * (width / nyq) + 7.95
            if atten > 50:
                beta = 0.1102 * (atten - 8.7)
            elif atten > 21:
                beta = 0.5842 * (atten - 21) ** 0.4 + 0.07886 * (atten - 21)
            else:
                beta = 0.0
            c = cutoff / nyq
            alpha = 0.5 * (numtaps - 1)
            m = np.arange(numtaps) - alpha
            h = c * np.sinc(c * m)
            h *= np.kaiser(numtaps, beta)
            h /= h.sum()
            return h.astype(np.float32)

        def _make_filter(size, factor):
            taps = FILTER_SIZE * factor
            f1d = _firwin_kaiser(taps, size / 2.0001, size, size)
            f2d = np.outer(f1d, f1d)[None, None]
            return jnp.asarray(f2d, dtype=jnp.float32)

        def _conv_same(x, f):
            k = f.shape[-1]
            pl = (k - 1) // 2
            pr = k - 1 - pl
            return jax.lax.conv_general_dilated(x, f, (1, 1), [(pl, pr), (pl, pr)])
        B, C, H, W = x.shape
        x = x + bias
        x = x.reshape(B * C, 1, H, W)
        x = jnp.repeat(jnp.repeat(x, UP_FACTOR, axis=2), UP_FACTOR, axis=3)
        x = _conv_same(x, up_filter)
        x = jax.nn.leaky_relu(x, negative_slope=SLOPE) * GAIN
        x = _conv_same(x, dn_filter)
        x = x[:, :, ::DN_FACTOR, ::DN_FACTOR]
        return x.reshape(B, C, OUT_SIZE, OUT_SIZE)

    def _L1_attn_ref(x, Wq, Wk, Wv):
        import jax, jax.numpy as jnp
        import numpy as np
        B, S, D = (4, 1024, 32)
        b, s, d = x.shape
        q = jnp.einsum('bsd,ed->bse', x, Wq)
        k = jnp.einsum('bsd,ed->bse', x, Wk)
        v = jnp.einsum('bsd,ed->bse', x, Wv)
        scores = jnp.einsum('bqd,bkd->bqk', q, k) / jnp.sqrt(jnp.float32(d))
        causal = jnp.tril(jnp.ones((s, s), dtype=bool))
        scores = jnp.where(causal, scores, jnp.float32(-jnp.inf))
        weights = jax.nn.softmax(scores.astype(jnp.float32), axis=-1)
        out = jnp.einsum('bqk,bkd->bqd', weights, v)
        return out

    def _L1_ffn_ref(x, gate_w, gate_b, weight1, weight2):
        import jax, jax.numpy as jnp
        import numpy as np
        B, S, D, E, H, O, K = (128, 512, 32, 16, 128, 32, 8)
        Bn, Sn, Dn = x.shape
        logits = jnp.einsum('bsd,ed->bse', x, gate_w) + gate_b
        probs = jax.nn.softmax(logits, axis=1)
        vals, idx = jax.lax.top_k(probs.transpose(0, 2, 1), K)
        topv = vals.transpose(0, 2, 1)
        topi = idx.transpose(0, 2, 1)
        flat_idx = topi.reshape(Bn, K * E)
        gathered = jnp.take_along_axis(x, flat_idx[:, :, None], axis=1)
        gathered = gathered.reshape(Bn, K, E, Dn)
        pooled = jnp.einsum('bked,bke->bed', gathered, topv)
        ones = jnp.ones((E, Bn, 1), dtype=x.dtype)
        h = jnp.concatenate([pooled.transpose(1, 0, 2), ones], axis=-1)
        h = jax.nn.gelu(jnp.einsum('ebd,edh->ebh', h, weight1), approximate=False)
        h = jnp.concatenate([h, ones], axis=-1)
        out = jnp.einsum('ebh,eho->ebo', h, weight2)
        out = out.transpose(1, 0, 2)
        weighted = jnp.einsum('beo,bke->bkeo', out, topv).reshape(Bn, K * E, O)
        outputs = jnp.zeros((Bn, Sn, O), dtype=x.dtype)
        outputs = outputs.at[jnp.arange(Bn)[:, None], flat_idx].add(weighted)
        return outputs

    def _gn(v, G=32, eps=1e-05):
        B_, H_, W_, C_ = v.shape
        g = v.reshape(B_, H_, W_, G, C_ // G)
        m = jnp.mean(g, axis=(1, 2, 4), keepdims=True)
        s = jnp.var(g, axis=(1, 2, 4), keepdims=True)
        return ((g - m) / jnp.sqrt(s + eps)).reshape(v.shape)

    def _ln_c(v, eps=1e-06):
        m = jnp.mean(v, axis=-1, keepdims=True)
        s = jnp.var(v, axis=-1, keepdims=True)
        return (v - m) / jnp.sqrt(s + eps)

    def _ln_t(v, eps=1e-05):
        m = jnp.mean(v, axis=-1, keepdims=True)
        s = jnp.var(v, axis=-1, keepdims=True)
        return (v - m) / jnp.sqrt(s + eps)

    def _to_tokens(v):
        B_, H_, W_, C_ = v.shape
        return v.reshape(B_, H_ * W_, C_)

    def _from_tokens(t, like):
        return t.reshape(like.shape)
    x = x + _L0_conv_ref(_gn(x), L0_conv_bias, L0_conv_up_filter, L0_conv_dn_filter)
    t = _to_tokens(x)
    t = t + _L1_attn_ref(_ln_t(t), L1_attn_Wq, L1_attn_Wk, L1_attn_Wv)
    t = t + _L1_ffn_ref(_ln_t(t), L1_ffn_gate_w, L1_ffn_gate_b, L1_ffn_weight1, L1_ffn_weight2)
    x = _from_tokens(t, x)
    return x

_drawn_inputs = setup_inputs


def setup_inputs(seed=0):
    import zlib

    import numpy as np

    out = dict(_drawn_inputs(seed))
    spreads = {'L0_conv_bias': (0.0, 0.1), 'L1_ffn_gate_b': (0.0, 0.1)}
    factors = {'L1_ffn_gate_w': 8.0, 'L1_ffn_weight1': 8.0, 'L1_ffn_weight2': 8.0}
    for name, (base, spread) in spreads.items():
        noise = np.random.default_rng([zlib.crc32(name.encode()), seed]).standard_normal(out[name].shape)
        drawn = base * np.exp(spread * noise) if base else spread * noise
        out[name] = jnp.asarray(drawn.astype(out[name].dtype))
    for name, factor in factors.items():
        out[name] = (out[name] * factor).astype(out[name].dtype)
    return out
```

```python
from contextlib import ExitStack

import numpy as np

import concourse.bass as bass
from concourse import mybir

F32 = mybir.dt.float32
BF16 = mybir.dt.bfloat16
ALU = mybir.AluOpType
ACT = mybir.ActivationFunctionType
X = mybir.AxisListType.X

B, H, W, C = 16, 32, 32, 32
S = H * W
P = 128
GB = P // C
G = B // GB
KT = S // P
TAPS = 12
PAD = (TAPS - 1) // 2
SHIFTS = [0, -1, 1, -2, 2, -3, 3]
NS = len(SHIFTS)
AROWS = 2 * NS + 1
TROW = 128
UP_AT, DN_AT = 58, 57
EW = 2 * W + 1
E_ = 16
HID = 128
GE = GB * E_
TOP = 8
HALF = 256
NEG = -1.0e30
SLOPE, GAIN = 0.2, float(np.sqrt(2.0))
EPS = 1e-5

POFF = [sum((KT - i) * P for i in range(j)) for j in range(KT)]
PCOLS = sum((KT - j) * P for j in range(KT))
SCORE_UNITS = [(i, c, min(HALF, (i + 1) * P - c * HALF)) for i in range(KT) for c in range(i // 2 + 1)]
PROB_UNITS = [(j, c, min(HALF, S - j * P - c * HALF)) for j in range(KT) for c in range((KT - j + 1) // 2)]
NU = len(SCORE_UNITS)

LOGITS_AT = 3

C_ID, C_Q, C_QREP, C_MASK, C_BD, C_BDE, C_SUM, C_COLS = 0, 128, 256, 384, 512, 516, 520, 524


def constants():
    q = np.zeros((C, C), np.float64)
    for i in range(C - 1):
        q[:i + 1, i] = 1.0 / np.sqrt((i + 1.0) * (i + 2.0))
        q[i + 1, i] = -(i + 1.0) / np.sqrt((i + 1.0) * (i + 2.0))
    t = np.zeros((P, C_COLS), np.float32)
    t[:, C_ID:C_ID + P] = np.eye(P)
    t[:, C_Q:C_Q + P] = np.kron(np.eye(GB), q)
    t[:C, C_QREP:C_QREP + P] = np.tile(q, (1, GB))
    t[:, C_MASK:C_MASK + P] = np.triu(np.full((P, P), NEG), 1)
    t[:, C_BD:C_BD + GB] = np.kron(np.eye(GB), np.ones((C, 1)))
    t[:GE, C_BDE:C_BDE + GB] = np.kron(np.eye(GB), np.ones((E_, 1)))
    t[C - 1::C, C_SUM:C_SUM + GB] = np.eye(GB)
    return t


def order():
    a = [("xT", g, 0) for g in range(G)] + [("small", 0, i) for i in range(3)] + [("dnT", 0, 0)]
    b = []
    for t in range(-1, G + 1):
        att, conv, route = 0 <= t < G, t + 1 < G, 0 <= t - 1
        if route:
            a += [("proj", t - 1, 0), ("proj", t - 1, 1)]
        if att:
            a += [("score", t, v) for v in range(NU)]
        if route:
            a += [("uT", t - 1, 0)]
        if att:
            a += [("shift", t, 0)]
        if conv:
            a += [("down", t + 1, 0)]
            b += [("up", t + 1, i) for i in range(4)]
        if route:
            a += [("wT", t - 1, 0), ("pool", t - 1, 0)]
        if conv:
            a += [("centred", t + 1, 0), ("zT", t + 1, 0)]
        if att:
            b += [("prob", t, v) for v in range(LOGITS_AT)]
        if route:
            b += [("logits", t - 1, 0)]
        if att:
            b += [("prob", t, v) for v in range(LOGITS_AT, NU)] + [("pv", t, 0), ("pv", t, 1)]
        if conv:
            b += [("tok", t + 1, 0), ("yT", t + 1, 0), ("yT", t + 1, 1)]
    a += [("o2", 0, 0), ("o2T", 0, 0)] + [("scatter", g, 0) for g in range(G)]
    b += [("hid", 0, 0)]
    return {u: n for n, u in enumerate(a)}, {u: n for n, u in enumerate(b)}


def hybrid_kernel(nc, x, bias, up_filter, dn_filter, Wq, Wk, Wv, gate_w, gate_b, weight1, weight2, out):
    x_tokens = x.rearrange("b h w c -> b (h w) c").rearrange("(g b) (p k) c -> g p b k c", g=G, k=KT)
    out_tokens = out.rearrange("b h w c -> b (h w) c").rearrange("(g b) (p k) c -> g p b k c", g=G, k=KT)
    cst_dram = nc.inline_tensor(constants(), name="shape_constants").ap()
    tables = nc.dram_tensor("filter_tables", (2, AROWS, TROW), F32, kind="Internal").ap()

    with ExitStack() as ctx:
        def sb(name, shape, dt=F32):
            return ctx.enter_context(nc.sbuf_tensor(name, shape, dt))

        def sem(name):
            return ctx.enter_context(nc.semaphore(name))

        cst = sb("cst", [P, C_COLS])
        ident = cst[:, C_ID:C_ID + P]
        ident16 = sb("ident16", [P, P], BF16)
        mask16 = sb("mask16", [P, P], BF16)
        x_all = sb("x_all", [P, G, GB * KT * C])
        xT_all = sb("xT_all", [P, G, S])
        xin = sb("xin", [P, S])
        biasr = sb("biasr", [P, H])
        stats = sb("stats", [P, G, 2, 6])
        mv = sb("mv", [P, G, 2])
        grstd = sb("grstd", [P, G])
        pads = sb("pads", [32, 2, TROW])
        dnrow = sb("dnrow", [32, TAPS])
        U = sb("U", [P, NS, 2, 2 * W])
        D = sb("D", [P, NS, C])
        y = sb("y", [P, GB, S])
        yflat = y[:, :, :].rearrange("p b s -> p (b s)")
        upE = yflat[:, 0:AROWS * EW].rearrange("p (a t) -> p a t", a=AROWS)
        upD = yflat[:, 1024:1024 + AROWS * 2 * W].rearrange("p (a t) -> p a t", a=AROWS)
        dnE = yflat[0:C, 2048:2048 + AROWS * 2 * W].rearrange("p (a t) -> p a t", a=AROWS)
        w1_sb = yflat[0:C + 1, 0:E_ * HID].rearrange("p (e h) -> p e h", e=E_)
        w2_sb = yflat[:, 2048:2048 + E_ * C].rearrange("p (e c) -> p e c", e=E_)
        w2b_sb = yflat[0:1, 3072:3072 + E_ * C].rearrange("p (e c) -> p e c", e=E_)
        tT = sb("tT", [P, S])
        z = sb("z", [P, KT, P])
        zT = sb("zT", [P, S])
        yT = sb("yT", [P, S])
        prob = sb("prob", [P, GB, PCOLS])
        x_by_tile = prob[:, 0, 0:G * S].rearrange("p (g k d) -> p g k d", g=G, k=KT)
        sq = sb("sq", [P, S])
        zss = sb("zss", [P, 32])
        uss = sb("uss", [P, 32])
        zrstd = sb("zrstd", [P, 32])
        urstd = sb("urstd", [P, 32])
        mpart = sb("mpart", [P, 2, GB, 4])
        negmax = sb("negmax", [P, KT, GB, C])
        oT = sb("oT", [P, S])
        t2_all = sb("t2_all", [P, G, S])
        rsum = sb("rsum", [P, KT, GB])
        nmean = sb("nmean", [P, 32])
        u = sb("u", [P, KT, P])
        uT = sb("uT", [P, S])
        att = uT[:, :].rearrange("p (k d) -> p k d", k=KT)
        lg = sb("lg", [GE, S])
        probs = sb("probs", [GE, S])
        rest = sb("rest", [GE, S])
        top8 = sb("top8", [GE, TOP])
        ntop = sb("ntop", [GE, 1])
        esum = sb("esum", [GE, 1])
        wT = sb("wT", [P, KT, GE])
        pooled = sb("pooled", [C + 1, E_, B])
        wq_sb = sb("wq_sb", [C, C])
        wk_sb = sb("wk_sb", [C, C])
        wv_sb = sb("wv_sb", [C, C])
        gw_sb = sb("gw_sb", [E_, GB, C])
        gb_sb = sb("gb_sb", [GE, 1])
        wvT = sb("wvT", [C, C])
        A_sb = sb("A_sb", [C, C])
        T1 = sb("T1", [C, GB, C])
        gateT = sb("gateT", [P, GB, E_])
        Vbd = sb("Vbd", [P, P + GB])
        Bbd = sb("Bbd", [P, GB, C])
        ones = sb("ones", [1, B])
        power = sb("power", [P, 1])
        hid = sb("hid", [HID, E_, B])
        o2 = sb("o2", [C, B, E_])
        obd = sb("obd", [GE, G, GB, C])

        psA = ctx.enter_context(nc.psum_tensor("psA", [P, 4, 512], F32))
        psB = ctx.enter_context(nc.psum_tensor("psB", [P, 4, 512], F32))
        A, Bu = order()

        def slotA(*unit):
            return psA[:, :, 0:HALF]

        def slotB(*unit):
            return psB[:, :, 0:HALF]

        x_loaded = [sem(f"x_loaded{g}") for g in range(G)]
        cst_loaded = sem("cst_loaded")
        proj_loaded = sem("proj_loaded")
        ffn_loaded = sem("ffn_loaded")
        filters_loaded = sem("filters_loaded")
        tables_stored = sem("tables_stored")
        toeplitz_loaded = sem("toeplitz_loaded")
        pads_zero = sem("pads_zero")
        fills_ready = sem("fills_ready")
        masks_ready = sem("masks_ready")
        a_filled, a_drained = sem("a_filled"), sem("a_drained")
        b_filled, b_drained = sem("b_filled"), sem("b_drained")
        up_ready = sem("up_ready")
        dn_reversed = sem("dn_reversed")
        xn_ready = sem("xn_ready")
        x_sorted = sem("x_sorted")
        xin_ready = sem("xin_ready")
        z_squared = sem("z_squared")
        y_ready = sem("y_ready")
        power_ready = sem("power_ready")
        max_ready = sem("max_ready")
        causal = sem("causal")
        t2_mean = sem("t2_mean")
        t2_centred = sem("t2_centred")
        t2_squared = sem("t2_squared")
        t2_var = sem("t2_var")
        t2_rstd = sem("t2_rstd")
        z_var, z_rstd = sem("z_var"), sem("z_rstd")
        g_var, g_rstd = sem("g_var"), sem("g_rstd")
        u_ready = sem("u_ready")
        lg_max = sem("lg_max")
        lg_exp = sem("lg_exp")
        route_ready = sem("route_ready")
        obd_ready = sem("obd_ready")
        result = sem("result")
        stored = sem("stored")
        dve_chain = sem("dve_chain")

        block = ctx.enter_context(nc.Block())

        @block.sync
        def _(sp):
            sp.dma_start(cst[:, :], cst_dram).then_inc(cst_loaded, 16)
            for g in range(G):
                sp.dma_start(x_all[:, g, :].rearrange("p (b k c) -> p b k c", b=GB, k=KT),
                             x_tokens[g]).then_inc(x_loaded[g], 16)
            sp.dma_start(wq_sb[:, :], Wq).then_inc(proj_loaded, 16)
            sp.dma_start(wk_sb[:, :], Wk).then_inc(proj_loaded, 16)
            sp.dma_start(wv_sb[:, :], Wv).then_inc(proj_loaded, 16)
            for b in range(GB):
                sp.dma_start(gw_sb[:, b, :], gate_w).then_inc(proj_loaded, 16)
                sp.dma_start(gb_sb[E_ * b:E_ * b + E_, :], gate_b.rearrange("(e a) -> e a", a=1)).then_inc(proj_loaded, 16)
            sp.wait_ge(a_filled, A["down", G - 1, 0] + 1)
            sp.dma_start(w1_sb[:, :, :], weight1.rearrange("e d h -> d e h")).then_inc(ffn_loaded, 16)
            sp.dma_start(w2_sb[:, :, :], weight2[:, 0:HID, :].rearrange("e h o -> h e o")).then_inc(ffn_loaded, 16)
            sp.dma_start(w2b_sb[:, :, :], weight2[:, HID:HID + 1, :].rearrange("e h o -> h e o")).then_inc(ffn_loaded, 16)
            for g in range(G):
                sp.wait_ge(result, g + 1)
                sp.dma_start(out_tokens[g], x_all[:, g, :].rearrange("p (b k c) -> p b k c", b=GB, k=KT)).then_inc(stored, 16)
            sp.wait_ge(stored, 16 * G)

        @block.gpsimd
        def _(pool):
            nc.gpsimd.memset(pads[:, :, :], 0.0).then_inc(pads_zero, 1)
            nc.gpsimd.memset(dnrow[:, :], 0.0).then_inc(pads_zero, 1)
            nc.gpsimd.memset(z[:, :, :], 1.0).then_inc(fills_ready, 1)
            nc.gpsimd.memset(negmax[:, :, :, :], 0.0).then_inc(fills_ready, 1)
            nc.gpsimd.memset(pooled[:, :, :], 1.0).then_inc(fills_ready, 1)
            nc.gpsimd.memset(ones[:, :], 1.0).then_inc(fills_ready, 1)
            nc.gpsimd.memset(power[:, :], -0.5).then_inc(power_ready, 1)
            pool.wait_ge(power_ready, 1)

            def inverse_root(v, n):
                return nc.gpsimd.tensor_tensor(v, v, power[:, 0:1].broadcast_to([P, n]), ALU.pow)

            def conv_input(g):
                pool.wait_ge(xn_ready, g + 1)
                if g == 0:
                    pool.wait_ge(filters_loaded, 48)
                else:
                    pool.wait_ge(b_filled, Bu["up", g - 1, 3] + 1)
                nc.gpsimd.tensor_tensor(xin[:, :].rearrange("p (h w) -> p h w", h=H),
                                        x_all[:, g, :].rearrange("p (h w) -> p h w", h=H),
                                        biasr[:, :].unsqueeze(2).broadcast_to([P, H, W]), ALU.add).then_inc(xin_ready, 1)

            def causal_blocks(g):
                for v, (j, c, N) in enumerate(PROB_UNITS):
                    if c == 0:
                        pool.wait_ge(b_drained, Bu["prob", g, v] + 1)
                        blk = prob[:, :, POFF[j]:POFF[j] + P]
                        nc.gpsimd.affine_select(out=blk, in_=blk, compare_op=ALU.is_ge, fill=0.0, base=0,
                                                pattern=[[0, GB], [1, P]], channel_multiplier=-1).then_inc(causal, 1)

            def centre(g):
                v = u[:, :, :].rearrange("p k (b c) -> p (k b) c", c=C)
                pool.wait_ge(t2_mean, g + 1)
                if g >= 1:
                    pool.wait_ge(a_filled, A["pool", g - 1, 0] + 1)
                nc.gpsimd.tensor_tensor(v, t2_all[:, g, :].rearrange("p (n c) -> p n c", c=C),
                                        nmean[:, :].unsqueeze(2).broadcast_to([P, 32, C]), ALU.add).then_inc(t2_centred, 1)
                pool.wait_ge(t2_var, g + 1)
                inverse_root(urstd[:, :], 32).then_inc(t2_rstd, 1)
                pool.wait_ge(t2_rstd, g + 1)
                nc.gpsimd.tensor_tensor(v, v, urstd[:, :].unsqueeze(2).broadcast_to([P, 32, C]), ALU.mult).then_inc(u_ready, 1)

            for g in range(G):
                pool.wait_ge(g_var, g + 1)
                inverse_root(grstd[:, g:g + 1], 1).then_inc(g_rstd, 1)
                if g == 0:
                    conv_input(0)
            for t in range(-1, G + 1):
                if t >= 1:
                    centre(t - 1)
                if t + 2 < G:
                    conv_input(t + 2)
                if 0 <= t < G:
                    causal_blocks(t)
                if t + 1 < G:
                    pool.wait_ge(z_var, t + 2)
                    inverse_root(zrstd[:, :], 32).then_inc(z_rstd, 1)

        @block.scalar
        def _(act):
            act.dma_start(biasr[:, :], bias.rearrange("a h c d -> a (h c d)").broadcast_to([P, H])).then_inc(filters_loaded, 16)
            act.wait_ge(pads_zero, 2)
            act.dma_start(pads[2:2 + TAPS, 0, UP_AT:UP_AT + TAPS], up_filter[0, 0]).then_inc(filters_loaded, 16)
            act.dma_start(dnrow[2:2 + TAPS, :], dn_filter[0, 0]).then_inc(filters_loaded, 16)
            act.wait_ge(filters_loaded, 48)
            act.wait_ge(dn_reversed, 1)
            act.dma_start(tables.rearrange("f a t -> a f t"), pads[0:AROWS, :, :]).then_inc(tables_stored, 16)
            act.wait_ge(tables_stored, 16)
            up_src = bass.AP(tensor=tables.tensor, offset=0, ap=[[2, C], [TROW, AROWS], [1, EW]])
            dn_src = bass.AP(tensor=tables.tensor, offset=AROWS * TROW, ap=[[2, C], [TROW, AROWS], [1, 2 * W]])
            for b in range(GB):
                act.dma_start(upE[C * b:C * b + C, :, :], up_src).then_inc(toeplitz_loaded, 16)
            act.dma_start(dnE[:, :, :], dn_src).then_inc(toeplitz_loaded, 16)

            for g in range(G):
                act.wait_ge(x_loaded[g], 16)
                nc.scalar.activation(x_by_tile[:, g].rearrange("p k (b c) -> p b k c", b=GB),
                                     x_all[:, g, :].rearrange("p (b k c) -> p b k c", b=GB, k=KT), ACT.Copy).then_inc(x_sorted, 1)

            def keep(g, i):
                act.wait_ge(b_filled, Bu["up", g, i] + 1)
                if i == 0 and g >= 1:
                    act.wait_ge(a_filled, A["down", g - 1, 0] + 1)
                nc.scalar.activation(y[:, :, HALF * i:HALF * i + HALF], slotB("up", g, i), ACT.Copy).then_inc(b_drained, 1)

            def exps(g, v):
                j, c, N = PROB_UNITS[v]
                o = POFF[j] + c * HALF
                act.wait_ge(b_filled, Bu["prob", g, v] + 1)
                nc.scalar.activation(prob[:, :, o:o + N], slotB("prob", g, v)[:, :, 0:N], ACT.Exp).then_inc(b_drained, 1)

            def logits(g):
                act.wait_ge(b_filled, Bu["logits", g, 0] + 1)
                act.wait_ge(proj_loaded, 16 * 11)
                nc.scalar.activation(lg[:, :].rearrange("p (a n) -> p a n", a=4), slotB("logits", g, 0)[0:GE],
                                     ACT.Identity, bias=gb_sb[:, 0:1]).then_inc(b_drained, 1)

            def exp_logits(g):
                act.wait_ge(lg_max, g + 1)
                nc.scalar.activation(probs[:, :], lg[:, :], ACT.Exp, bias=ntop[:, 0:1],
                                     accum_out=esum[:, 0:1]).then_inc(lg_exp, 1)

            def halves(dst, name, g, i):
                act.wait_ge(b_filled, Bu[name, g, i] + 1)
                nc.scalar.activation(dst[:, 512 * i:512 * i + 512].rearrange("p (a n) -> p a n", a=2),
                                     slotB(name, g, i)[:, 2 * i:2 * i + 2], ACT.Copy).then_inc(b_drained, 1)

            for t in range(-1, G + 1):
                if t - 1 >= 0:
                    act.wait_ge(t2_centred, t)
                    nc.scalar.activation(sq[:, :], u[:, :, :].rearrange("p k d -> p (k d)"), ACT.Square).then_inc(t2_squared, 1)
                if t + 1 < G:
                    for i in range(4):
                        keep(t + 1, i)
                if 0 <= t < G:
                    for v in range(NU):
                        if v == LOGITS_AT and t >= 1:
                            logits(t - 1)
                        if v == LOGITS_AT + 6 and t >= 1:
                            exp_logits(t - 1)
                        exps(t, v)
                    for i in range(2):
                        halves(oT, "pv", t, i)
                elif t == G:
                    logits(t - 1)
                    exp_logits(t - 1)
                if t + 1 < G:
                    act.wait_ge(a_filled, A["centred", t + 1, 0] + 1)
                    if t >= 1:
                        act.wait_ge(t2_rstd, t)
                    nc.scalar.activation(sq[:, :].rearrange("p (a n) -> p a n", a=4), slotA("centred", t + 1, 0),
                                         ACT.Square).then_inc(z_squared, 1)
                    act.wait_ge(b_filled, Bu["tok", t + 1, 0] + 1)
                    nc.scalar.activation(t2_all[:, t + 1, :].rearrange("p (a n) -> p a n", a=4), slotB("tok", t + 1, 0),
                                         ACT.Copy).then_inc(b_drained, 1)
                    for i in range(2):
                        halves(yT, "yT", t + 1, i)
            act.wait_ge(b_filled, Bu["hid", 0, 0] + 1)
            nc.scalar.activation(hid[:, :, :], slotB("hid", 0, 0)[:, 0, :].rearrange("p (e b) -> p e b", e=E_),
                                 ACT.Gelu).then_inc(b_drained, 1)

        @block.vector
        def _(dve):
            chained = [0]

            def link(ins):
                chained[0] += 1
                ins.then_inc(dve_chain, 1)
                dve.wait_ge(dve_chain, chained[0])

            def filled(*unit):
                dve.wait_ge(a_filled, A[unit] + 1)
                return slotA(*unit)

            def group_norm(g):
                src = filled("xT", g, 0).rearrange("p a (e q) -> p a e q", e=2)
                dst = xT_all[:, g, :].rearrange("p (q a e) -> p a e q", a=4, e=2)
                nc.vector.tensor_copy(dst, src).then_inc(a_drained, 1)
                dve.wait_ge(a_drained, A["xT", g, 0] + 1)
                for i in range(2):
                    link(nc.vector.bn_stats(stats[:, g, i, :], xT_all[:, g, 512 * i:512 * i + 512]))
                link(nc.vector.bn_aggr(mv[:, g, :], stats[:, g, :, :].rearrange("p a s -> p (a s)")))
                nc.vector.tensor_scalar(grstd[:, g:g + 1], mv[:, g, 1:2], EPS, None, ALU.add).then_inc(g_var, 1)
                dve.wait_ge(g_rstd, g + 1)
                nc.vector.tensor_scalar(x_all[:, g, :], xT_all[:, g, :], mv[:, g, 0:1], grstd[:, g:g + 1],
                                        ALU.subtract, ALU.mult).then_inc(xn_ready, 1)

            dve.wait_ge(filters_loaded, 48)
            nc.vector.tensor_copy(pads[:, 1, DN_AT:DN_AT + TAPS], dnrow[:, ::-1]).then_inc(dn_reversed, 1)
            dve.wait_ge(cst_loaded, 16)
            nc.vector.tensor_copy(ident16[:, :], ident).then_inc(masks_ready, 1)
            nc.vector.tensor_copy(mask16[:, :], cst[:, C_MASK:C_MASK + P]).then_inc(masks_ready, 1)
            for g in range(G):
                group_norm(g)

            s = filled("small", 0, 0)
            link(nc.vector.tensor_copy(wvT[:, :], s[0:C, 0, 0:C]))
            link(nc.vector.tensor_copy(A_sb[:, :], s[0:C, 1, 0:C]))
            nc.vector.tensor_tensor(gateT[:, :, :], s[:, 2, 0:E_].unsqueeze(1).broadcast_to([P, GB, E_]),
                                    cst[:, C_BD:C_BD + GB].unsqueeze(2).broadcast_to([P, GB, E_]), ALU.mult).then_inc(a_drained, 1)
            s = filled("small", 0, 1)
            link(nc.vector.tensor_copy(T1[:, :, :], s[0:C, 0, 0:C].unsqueeze(1).broadcast_to([C, GB, C])))
            link(nc.vector.tensor_copy(Vbd[:, P:P + GB], cst[:, C_SUM:C_SUM + GB]))
            nc.vector.tensor_tensor(Vbd[:, 0:P].rearrange("p (b c) -> p b c", b=GB), s[:, 1, 0:C].unsqueeze(1).broadcast_to([P, GB, C]),
                                    cst[:, C_BD:C_BD + GB].unsqueeze(2).broadcast_to([P, GB, C]), ALU.mult).then_inc(a_drained, 1)
            s = filled("small", 0, 2)
            link(nc.vector.tensor_scalar(Bbd[:, :, :], s[:, 0, 0:C].unsqueeze(1).broadcast_to([P, GB, C]),
                                         float(C) ** -0.5, None, ALU.mult))
            nc.vector.tensor_tensor(Bbd[:, :, :], Bbd[:, :, :],
                                    cst[:, C_BD:C_BD + GB].unsqueeze(2).broadcast_to([P, GB, C]), ALU.mult).then_inc(a_drained, 1)

            dve.wait_ge(toeplitz_loaded, 16 * 5)
            link(nc.vector.tensor_tensor(upD[:, :, :], upE[:, :, 0:2 * W], upE[:, :, 1:2 * W + 1], ALU.add))
            nc.vector.tensor_tensor(U[:, :, 0, :], upD[:, 1:2 * NS:2, :], upD[:, 2:2 * NS + 1:2, :], ALU.add).then_inc(up_ready, 1)
            nc.vector.tensor_tensor(U[:, :, 1, :], upD[:, 0:2 * NS - 1:2, :], upD[:, 1:2 * NS:2, :], ALU.add).then_inc(up_ready, 1)
            s = filled("dnT", 0, 0)
            nc.vector.tensor_copy(D[:, :, :], s[:, 0, 0:NS * C].rearrange("p (m c) -> p m c", m=NS)).then_inc(a_drained, 1)
            dve.wait_ge(fills_ready, 4)

            def attention_out(g):
                for p in range(2):
                    s = filled("proj", g, p)
                    link(nc.vector.reciprocal(rsum[:, 4 * p:4 * p + 4, :], s[:, :, P:P + GB]))
                    nc.vector.tensor_tensor(att[:, 4 * p:4 * p + 4, :].rearrange("p k (b c) -> p k b c", b=GB),
                                            s[:, :, 0:P].rearrange("p k (b c) -> p k b c", b=GB),
                                            rsum[:, 4 * p:4 * p + 4, :].unsqueeze(3).broadcast_to([P, 4, GB, C]),
                                            ALU.mult).then_inc(a_drained, 1)
                dve.wait_ge(a_drained, A["proj", g, 1] + 1)
                dve.wait_ge(b_drained, Bu["tok", g, 0] + 1)
                link(nc.vector.tensor_tensor(t2_all[:, g, :], t2_all[:, g, :], att[:, :, :].rearrange("p k d -> p (k d)"), ALU.add))
                link(nc.vector.tensor_reduce(nmean[:, :], t2_all[:, g, :].rearrange("p (n c) -> p n c", c=C), X, ALU.add))
                nc.vector.tensor_scalar(nmean[:, :], nmean[:, :], -1.0 / C, None, ALU.mult).then_inc(t2_mean, 1)

            def deviation(g):
                dve.wait_ge(t2_squared, g + 1)
                link(nc.vector.tensor_reduce(uss[:, :], sq[:, :].rearrange("p (n c) -> p n c", c=C), X, ALU.add))
                nc.vector.tensor_scalar(urstd[:, :], uss[:, :], 1.0 / C, EPS, ALU.mult, ALU.add).then_inc(t2_var, 1)

            def score_max(g, v):
                i, c, N = SCORE_UNITS[v]
                s = filled("score", g, v)[:, :, 0:N]
                last = c == i // 2
                if last and c == 0:
                    nc.vector.tensor_reduce(negmax[:, i, :, C - 1], s, X, ALU.max, negate=True).then_inc(a_drained, 1)
                    return
                nc.vector.tensor_reduce(mpart[:, i % 2, :, c], s, X, ALU.max).then_inc(a_drained, 1)
                if last:
                    dve.wait_ge(a_drained, A["score", g, v] + 1)
                    ins = nc.vector.tensor_reduce(negmax[:, i, :, C - 1], mpart[:, i % 2, :, 0:c + 1], X, ALU.max, negate=True)
                    if i == KT - 1:
                        ins.then_inc(max_ready, 1)

            def leaky(g, i):
                v = y[:, :, HALF * i:HALF * i + HALF]
                dve.wait_ge(b_drained, Bu["up", g, i] + 1)
                nc.vector.scalar_tensor_tensor(out=v, in0=v, scalar=SLOPE, in1=v, op0=ALU.mult, op1=ALU.max).then_inc(y_ready, 1)

            def route_max(g):
                dve.wait_ge(b_drained, Bu["logits", g, 0] + 1)
                link(nc.vector.max(top8[:, :], lg[:, :]))
                nc.vector.tensor_scalar(ntop[:, :], top8[:, 0:1], -1.0, None, ALU.mult).then_inc(lg_max, 1)

            def route(g):
                dve.wait_ge(lg_exp, g + 1)
                link(nc.vector.reciprocal(esum[:, :], esum[:, :]))
                link(nc.vector.tensor_scalar(probs[:, :], probs[:, :], esum[:, 0:1], None, ALU.mult))
                link(nc.vector.max(top8[:, :], probs[:, :]))
                link(nc.vector.match_replace(rest[:, :], top8[:, :], probs[:, :], 0.0))
                nc.vector.tensor_tensor(xT_all[0:GE, g, :], probs[:, :], rest[:, :], ALU.subtract).then_inc(route_ready, 1)

            for t in range(-1, G + 1):
                att_on, conv_on, route_on = 0 <= t < G, t + 1 < G, t >= 1
                if route_on:
                    attention_out(t - 1)
                leaks = iter(range(4 if conv_on else 0))
                if att_on:
                    for v in range(NU):
                        if v == 4 and route_on:
                            deviation(t - 1)
                        score_max(t, v)
                        if (6 + v + 1 + (v + 1) // 8) // NS > (6 + v + v // 8) // NS:
                            for i in leaks:
                                leaky(t + 1, i)
                                break
                elif route_on:
                    deviation(t - 1)
                for i in leaks:
                    leaky(t + 1, i)
                if route_on:
                    src = filled("uT", t - 1, 0).rearrange("p a (e q) -> p a e q", e=2)
                    nc.vector.tensor_copy(uT[:, :].rearrange("p (q a e) -> p a e q", a=4, e=2), src).then_inc(a_drained, 1)
                if att_on:
                    s = filled("shift", t, 0)
                    v4 = yT[:, :].rearrange("p (a n) -> p a n", a=4)
                    nc.vector.tensor_tensor(v4, v4, s, ALU.add).then_inc(a_drained, 1)
                if route_on:
                    route_max(t - 1)
                if conv_on:
                    s = filled("down", t + 1, 0)
                    nc.vector.scalar_tensor_tensor(out=tT[:, :].rearrange("p (a n) -> p a n", a=4), in0=s, scalar=GAIN,
                                                   in1=xT_all[:, t + 1, :].rearrange("p (a n) -> p a n", a=4),
                                                   op0=ALU.mult, op1=ALU.add).then_inc(a_drained, 1)
                if route_on:
                    g = t - 1
                    route(g)
                    s = filled("wT", g, 0)
                    nc.vector.tensor_copy(wT[:, :, :].rearrange("p (a e) n -> p a e n", e=2),
                                          s[:, :, 0:2 * GE].rearrange("p a (e n) -> p a e n", e=2)).then_inc(a_drained, 1)
                    s = filled("pool", g, 0)
                    for b in range(GB):
                        ins = nc.vector.tensor_copy(pooled[0:C, :, GB * g + b], s[C * b:C * b + C, 0, E_ * b:E_ * b + E_])
                    ins.then_inc(a_drained, 1)
                if conv_on:
                    g = t + 1
                    s = filled("centred", g, 0).rearrange("p a (n c) -> p a n c", c=C)
                    dve.wait_ge(z_squared, g + 1)
                    link(nc.vector.tensor_reduce(zss[:, :], sq[:, :].rearrange("p (n c) -> p n c", c=C), X, ALU.add))
                    nc.vector.tensor_scalar(zrstd[:, :], zss[:, :], 1.0 / C, EPS, ALU.mult, ALU.add).then_inc(z_var, 1)
                    dve.wait_ge(z_rstd, g + 1)
                    nc.vector.tensor_tensor(z[:, :, :].rearrange("p (a k) (b c) -> p a (k b) c", a=4, c=C)[:, :, :, 0:C - 1],
                                            s[:, :, :, 0:C - 1],
                                            zrstd[:, :].rearrange("p (a n) -> p a n", a=4).unsqueeze(3).broadcast_to([P, 4, 8, C - 1]),
                                            ALU.mult).then_inc(a_drained, 1)
                    s = filled("zT", g, 0)
                    nc.vector.tensor_copy(zT[:, :].rearrange("p (a n) -> p a n", a=4), s).then_inc(a_drained, 1)

            s = filled("o2", 0, 0)
            nc.vector.tensor_copy(o2[:, :, :], s[0:C, 0, :].rearrange("p (b e) -> p b e", b=B)).then_inc(a_drained, 1)
            s = filled("o2T", 0, 0)
            for g in range(G):
                ins = nc.vector.tensor_tensor(obd[:, g, :, :], s[0:GE, g, 0:C].unsqueeze(1).broadcast_to([GE, GB, C]),
                                              cst[0:GE, C_BDE:C_BDE + GB].unsqueeze(2).broadcast_to([GE, GB, C]), ALU.mult)
            ins.then_inc(a_drained, 1)
            for g in range(G):
                s = filled("scatter", g, 0).rearrange("p a (e b c) -> p a e b c", e=2, b=GB)
                t2v = t2_all[:, g, :].rearrange("p (a e b c) -> p a e b c", a=4, e=2, b=GB)
                ov = x_all[:, g, :].rearrange("p (b a e c) -> p a e b c", b=GB, a=4, e=2)
                for e in range(2):
                    ins = nc.vector.tensor_tensor(ov[:, :, e], s[:, :, e], t2v[:, :, e], ALU.add)
                    if e == 0:
                        continue
                    ins.then_inc(result, 1)

        @block.tensor
        def _(pe):
            def slot_a(*unit):
                if A[unit] >= 1:
                    pe.wait_ge(a_drained, A[unit])
                return slotA(*unit)

            def slot_b(*unit):
                if Bu[unit] >= 1:
                    pe.wait_ge(b_drained, Bu[unit])
                return slotB(*unit)

            def turn(s, src):
                for k in range(KT):
                    ins = nc.tensor.transpose(s[:, k // 2, k % 2 * P:k % 2 * P + P], src(k), ident)
                return ins

            pe.wait_ge(cst_loaded, 16)
            for g in range(G):
                pe.wait_ge(x_sorted, g + 1)
                turn(slot_a("xT", g, 0), lambda k: x_by_tile[:, g, k, :]).then_inc(a_filled, 1)

            pe.wait_ge(proj_loaded, 16 * 11)
            s = slot_a("small", 0, 0)
            nc.tensor.matmul(s[0:C, 0, 0:C], wv_sb[:, :], ident[0:C, 0:C], start=True, stop=True)
            nc.tensor.matmul(s[0:C, 1, 0:C], wq_sb[:, :], wk_sb[:, :], start=True, stop=True)
            nc.tensor.matmul(s[:, 2, 0:E_], gw_sb[:, :, :], ident[0:E_, 0:E_], start=True, stop=True).then_inc(a_filled, 1)
            s = slot_a("small", 0, 1)
            pe.wait_ge(a_drained, A["small", 0, 0] + 1)
            nc.tensor.matmul(s[0:C, 0, 0:C], A_sb[:, :], cst[0:C, C_Q:C_Q + C], start=True, stop=True)
            nc.tensor.matmul(s[:, 1, 0:C], cst[0:C, C_QREP:C_QREP + P], wvT[:, :], start=True, stop=True).then_inc(a_filled, 1)
            s = slot_a("small", 0, 2)
            pe.wait_ge(a_drained, A["small", 0, 1] + 1)
            nc.tensor.matmul(s[:, 0, 0:C], T1[:, :, :], cst[0:C, C_Q:C_Q + C], start=True, stop=True).then_inc(a_filled, 1)
            pe.wait_ge(toeplitz_loaded, 16 * 5)
            s = slot_a("dnT", 0, 0)
            dn_flat = dnE.rearrange("p a t -> p (a t)")
            for m in range(NS):
                ins = nc.tensor.matmul(s[:, 0, C * m:C * m + C], dn_flat[:, 2 * W * (2 * m + 1):2 * W * (2 * m + 3)], ident[0:C, 0:C], start=True, stop=True)
            ins.then_inc(a_filled, 1)
            pe.wait_ge(masks_ready, 2)
            pe.wait_ge(fills_ready, 4)
            pe.wait_ge(up_ready, 2)

            def part(v, m):
                return v[:, :, max(0, m):W + min(0, m)]

            def up_pieces(g):
                for i in range(4):
                    for n, m in enumerate(SHIFTS):
                        if n == 0:
                            s = slot_b("up", g, i)
                            if i == 0:
                                pe.wait_ge(xin_ready, g + 1)
                        for b in range(GB):
                            xv = xin[C * b:C * b + C, HALF * i:HALF * i + HALF].rearrange("p (h w) -> p h w", w=W)
                            ins = nc.tensor.matmul(part(s[:, b].rearrange("p (h w) -> p h w", w=W), -m),
                                                   U[C * b:C * b + C, m + 3, :, :], part(xv, m),
                                                   start=n == 0, stop=n == NS - 1)
                        if n == NS - 1:
                            ins.then_inc(b_filled, 1)
                        yield

            def down_pieces(g):
                s = slot_a("down", g, 0)
                pe.wait_ge(y_ready, 4 * (g + 1))
                if g == 0:
                    pe.wait_ge(a_drained, A["dnT", 0, 0] + 1)
                for i in range(4):
                    for n, m in enumerate(SHIFTS):
                        for b in range(GB):
                            yv = y[:, b, HALF * i:HALF * i + HALF].rearrange("p (h w) -> p h w", w=W)
                            ov = s[C * b:C * b + C, i].rearrange("p (h w) -> p h w", w=W)
                            ins = nc.tensor.matmul(part(ov, -m), D[:, m + 3, :], part(yv, m),
                                                   start=n == 0, stop=n == NS - 1)
                        if i == 3 and n == NS - 1:
                            ins.then_inc(a_filled, 1)
                        yield

            def score(g, v):
                i, c, N = SCORE_UNITS[v]
                s = slot_a("score", g, v)
                diagonal = c == i // 2
                if v == 0:
                    pe.wait_ge(a_drained, A["zT", g, 0] + 1)
                    pe.wait_ge(b_drained, Bu["yT", g, 1] + 1)
                for b in range(GB):
                    r = slice(C * b, C * b + C)
                    ins = nc.tensor.matmul(s[:, b, 0:N], yT[r, P * i:P * i + P], zT[r, c * HALF:c * HALF + N],
                                           start=True, stop=not diagonal)
                if diagonal:
                    for b in range(GB):
                        ins = nc.tensor.matmul(s[:, b, N - P:N], ident16[:, :], mask16[:, :], start=False, stop=True)
                ins.then_inc(a_filled, 1)

            def prob_scores(g, v):
                j, c, N = PROB_UNITS[v]
                s = slot_b("prob", g, v)
                q = P * j + HALF * c
                if v == 0:
                    pe.wait_ge(a_drained, A["shift", g, 0] + 1)
                for b in range(GB):
                    r = slice(C * b, C * b + C)
                    ins = nc.tensor.matmul(s[:, b, 0:N], zT[r, P * j:P * j + P], yT[r, q:q + N], start=True, stop=True)
                ins.then_inc(b_filled, 1)

            def weighted(g):
                for i in range(2):
                    s = slot_b("pv", g, i)
                    if i == 0:
                        pe.wait_ge(b_drained, Bu["prob", g, NU - 1] + 1)
                        pe.wait_ge(causal, KT * (g + 1))
                    for a in (2 * i, 2 * i + 1):
                        for j in range(2 * a + 2):
                            lo = max(P * j, HALF * a)
                            for b in range(GB):
                                o = POFF[j] + lo - P * j
                                N = HALF * a + HALF - lo
                                ins = nc.tensor.matmul(s[C * b:C * b + C, a, HALF - N:HALF], z[:, j, C * b:C * b + C],
                                                       prob[:, b, o:o + N], start=j == 0, stop=j == 2 * a + 1)
                    ins.then_inc(b_filled, 1)

            def project(g):
                for p in range(2):
                    s = slot_a("proj", g, p)
                    pe.wait_ge(b_drained, Bu["pv", g, 1] + 1)
                    ov = oT[:, :].rearrange("p (q k) -> p k q", k=KT)
                    for k in range(4):
                        ins = nc.tensor.matmul(s[:, k, 0:P + GB], ov[:, 4 * p + k, :], Vbd[:, :], start=True, stop=True)
                    ins.then_inc(a_filled, 1)

            def logits(g):
                s = slot_b("logits", g, 0)
                pe.wait_ge(a_drained, A["uT", g, 0] + 1)
                for a in range(4):
                    ins = nc.tensor.matmul(s[0:GE, a], gateT[:, :, :], uT[:, HALF * a:HALF * a + HALF], start=True, stop=True)
                ins.then_inc(b_filled, 1)

            def pool_tokens(g):
                s = slot_a("wT", g, 0)
                pe.wait_ge(route_ready, g + 1)
                wv = xT_all[0:GE, g, :].rearrange("p (q k) -> p k q", k=KT)
                for k in range(KT):
                    ins = nc.tensor.transpose(s[:, k // 2, k % 2 * GE:k % 2 * GE + GE], wv[:, k, :], ident[0:GE, 0:GE])
                ins.then_inc(a_filled, 1)
                s = slot_a("pool", g, 0)
                pe.wait_ge(a_drained, A["wT", g, 0] + 1)
                for k in range(KT):
                    ins = nc.tensor.matmul(s[:, 0, 0:GE], u[:, k, :], wT[:, k, :], start=k == 0, stop=k == KT - 1)
                ins.then_inc(a_filled, 1)

            def tokens(g):
                s = slot_a("centred", g, 0)
                pe.wait_ge(a_drained, A["down", g, 0] + 1)
                for k in range(KT):
                    ins = nc.tensor.matmul(s[:, k // 2, k % 2 * P:k % 2 * P + P], tT[:, P * k:P * k + P],
                                           cst[:, C_Q:C_Q + P], start=True, stop=True)
                ins.then_inc(a_filled, 1)
                tv = tT[:, :].rearrange("p (q k) -> p k q", k=KT)
                turn(slot_b("tok", g, 0), lambda k: tv[:, k, :]).then_inc(b_filled, 1)
                s = slot_a("zT", g, 0)
                pe.wait_ge(a_drained, A["centred", g, 0] + 1)
                turn(s, lambda k: z[:, k, :]).then_inc(a_filled, 1)
                for i in range(2):
                    s = slot_b("yT", g, i)
                    pe.wait_ge(a_drained, A["zT", g, 0] + 1)
                    for a in (2 * i, 2 * i + 1):
                        ins = nc.tensor.matmul(s[:, a], Bbd[:, :, :], zT[:, HALF * a:HALF * a + HALF], start=True, stop=True)
                    ins.then_inc(b_filled, 1)

            def take(pieces, n):
                for _ in range(n):
                    next(pieces, None)

            for t in range(-1, G + 1):
                att_on, conv_on, route_on = 0 <= t < G, t + 1 < G, t >= 1
                if route_on:
                    project(t - 1)
                up = up_pieces(t + 1) if conv_on else iter(())
                take(up, 6 if att_on else 4 * NS)
                if att_on:
                    for v in range(NU):
                        score(t, v)
                        take(up, 1 + (v % 8 == 7))
                take(up, 4 * NS)
                if route_on:
                    pe.wait_ge(u_ready, t)
                    turn(slot_a("uT", t - 1, 0), lambda k: u[:, k, :]).then_inc(a_filled, 1)
                if att_on:
                    s = slot_a("shift", t, 0)
                    pe.wait_ge(max_ready, t + 1)
                    turn(s, lambda k: negmax[:, k, :, :]).then_inc(a_filled, 1)
                down = down_pieces(t + 1) if conv_on else iter(())
                if att_on:
                    for v in range(NU):
                        if v == LOGITS_AT and route_on:
                            logits(t - 1)
                        prob_scores(t, v)
                        take(down, 1 + (v % 2))
                elif route_on:
                    logits(t - 1)
                take(down, 4 * NS)
                if route_on:
                    pool_tokens(t - 1)
                if att_on:
                    weighted(t)
                if conv_on:
                    tokens(t + 1)

            pe.wait_ge(ffn_loaded, 48)
            s = slot_b("hid", 0, 0)
            pe.wait_ge(a_drained, A["pool", G - 1, 0] + 1)
            for e in range(E_):
                ins = nc.tensor.matmul(s[:, 0, B * e:B * e + B], w1_sb[:, e, :], pooled[:, e, :], start=True, stop=True)
            ins.then_inc(b_filled, 1)
            s = slot_a("o2", 0, 0)
            pe.wait_ge(b_drained, Bu["hid", 0, 0] + 1)
            sv = s[0:C, 0, :].rearrange("p (b e) -> p e b", b=B)
            for e in range(E_):
                nc.tensor.matmul(sv[:, e, :], w2_sb[:, e, :], hid[:, e, :], start=True, stop=False)
                ins = nc.tensor.matmul(sv[:, e, :], w2b_sb[:, e, :], ones[:, :], start=False, stop=True)
            ins.then_inc(a_filled, 1)
            s = slot_a("o2T", 0, 0)
            pe.wait_ge(a_drained, A["o2", 0, 0] + 1)
            for g in range(G):
                ins = nc.tensor.transpose(s[0:GE, g, 0:C], o2[:, GB * g:GB * g + GB, :], ident[0:C, 0:C])
            ins.then_inc(a_filled, 1)
            for g in range(G):
                s = slot_a("scatter", g, 0) if g < 1 else slotA("scatter", g, 0)
                if g >= 1:
                    pe.wait_ge(result, g)
                pe.wait_ge(a_drained, A["o2T", 0, 0] + 1)
                wv = xT_all[0:GE, g, :].rearrange("p (q k) -> p k q", k=KT)
                for k in range(KT):
                    ins = nc.tensor.matmul(s[:, k // 2, k % 2 * P:k % 2 * P + P], wv[:, k, :], obd[:, g, :, :], start=True, stop=True)
                ins.then_inc(a_filled, 1)


_INS = ['x', 'L0_conv_bias', 'L0_conv_up_filter', 'L0_conv_dn_filter', 'L1_attn_Wq', 'L1_attn_Wk', 'L1_attn_Wv',
        'L1_ffn_gate_w', 'L1_ffn_gate_b', 'L1_ffn_weight1', 'L1_ffn_weight2']
_OUTS = [((16, 32, 32, 32), 'float32')]


def kernel(**inputs):
    import numpy as _np
    import concourse.bacc as _bacc
    from concourse import mybir as _mybir
    from concourse.bass_utils import run_bass_kernel_spmd as _run

    nc = _bacc.Bacc("TRN2", target_bir_lowering=False, num_devices=1)
    arrays, args = {}, []
    for name in _INS:
        a = _np.ascontiguousarray(inputs[name])
        arrays[f"in_{name}_dram"] = a
        args.append(nc.dram_tensor(f"in_{name}_dram", a.shape, _mybir.dt.from_np(a.dtype), kind="ExternalInput").ap())
    for i, (shape, dtype) in enumerate(_OUTS):
        dt = _mybir.dt.from_np(_np.dtype(dtype))
        args.append(nc.dram_tensor(f"out_{i}_dram", shape, dt, kind="ExternalOutput").ap())
    hybrid_kernel(nc, *args)
    r = _run(nc, [arrays], core_ids=[0])
    return r.results[0]["out_0_dram"]
```

```python
from contextlib import ExitStack

import numpy as np

import concourse.bass as bass
from concourse import mybir

F32 = mybir.dt.float32
F16 = mybir.dt.float16
BF16 = mybir.dt.bfloat16
ALU = mybir.AluOpType
ACT = mybir.ActivationFunctionType
X = mybir.AxisListType.X

B, H, W, C = 16, 32, 32, 32
S = H * W
P = 128
R = P // C
JW = W // R
BC = H * JW
GB = 4
G = B // GB
KT = S // P
HB = KT // R
TAPS = 12
NS = 7
SPAN = NS + R - 1
AROWS = 2 * NS + 1
TROW = 128
UP_AT, DN_AT = 58, 57
EW = 2 * W + 1
E_ = 16
HID = 128
GE = GB * E_
TOP = 8
SLOT = 1024
BANK = 512
NEG = -1.0e30
SLOPE, GAIN = 0.2, float(np.sqrt(2.0))
EPS = 1e-5

PACK = [[8], [7, 1], [6, 2], [5, 3], [4]]
NU = len(PACK)


def packed(u):
    at, out = 0, []
    for n in PACK[u]:
        out.append((n, at))
        at += n * P
    return out


UCOLS = [sum(p) * P for p in PACK]
UOFF = [sum(UCOLS[:u]) for u in range(NU)]
PCOLS = sum(UCOLS)
PLACE = {KT - n: UOFF[u] + at for u in range(NU) for n, at in packed(u)}

C_ID, C_Q, C_QREP, C_MASK, C_AVG, C_BD, C_BDE, C_HALF, C_SUM, C_COLS = 0, 128, 256, 384, 512, 640, 644, 648, 650, 652


def constants():
    q = np.zeros((C, C), np.float64)
    for i in range(C - 1):
        q[:i + 1, i] = 1.0 / np.sqrt((i + 1.0) * (i + 2.0))
        q[i + 1, i] = -(i + 1.0) / np.sqrt((i + 1.0) * (i + 2.0))
    t = np.zeros((P, C_COLS), np.float32)
    t[:, C_ID:C_ID + P] = np.eye(P)
    t[:, C_Q:C_Q + P] = np.kron(np.eye(R), q)
    t[:C, C_QREP:C_QREP + P] = np.tile(q, (1, R))
    t[:, C_MASK:C_MASK + P] = np.triu(np.full((P, P), NEG), 1)
    t[:, C_AVG:C_AVG + P] = np.tile(np.eye(C), (R, R)) / R
    t[:, C_BD:C_BD + GB] = np.kron(np.eye(GB), np.ones((C, 1)))
    t[:GE, C_BDE:C_BDE + GB] = np.kron(np.eye(GB), np.ones((E_, 1)))
    t[:, C_HALF:C_HALF + 2] = np.kron(np.eye(2), np.ones((2 * C, 1)))
    t[C - 1::C, C_SUM:C_SUM + 2] = np.kron(np.eye(2), np.ones((2, 1)))
    return t


def schedule():
    ev = [("xT", 0), ("small", 0), ("gn_mean", 0), ("small", 1), ("gn_var", 0), ("small", 2), ("xT", 1), ("normalise", 0),
          ("xT", 2), ("xT", 3), ("dnT", 0), ("gn_mean", 1), ("gn_var", 1), ("normalise", 1)]
    for t in range(-7, B + 6):
        def on(n):
            return 0 <= n < B

        def put(batch, *e):
            if on(batch):
                ev.append(e)

        g5, g6, g7, g8 = ((t - k) // GB if (t - k) % GB == 0 and on(t - k) else None for k in (5, 6, 7, 8))
        if g5 is not None:
            ev += [("proj", g5, 0), ("proj", g5, 1), ("mean", g5)]
        put(t + 1, "score", t + 1, 0)
        put(t, "shift", t)
        if g5 is not None:
            ev.append(("dev", g5))
        if g7 is not None:
            ev += [("logit_exp", g7)]
        put(t + 7, "up", t + 7)
        put(t, "prob", t, 0)
        if g6 is not None:
            ev += [("uT", g6)]
        if g7 is not None:
            ev += [("route", g7)]
        put(t + 1, "score", t + 1, 1)
        put(t, "prob", t, 1)
        put(t, "low", t, 0)
        if g6 is not None:
            ev += [("logits", g6)]
        put(t + 7, "leak", t + 7)
        put(t - 1, "pv", t - 1)
        put(t + 1, "score", t + 1, 2)
        put(t, "prob", t, 2)
        put(t, "low", t, 1)
        if g6 is not None:
            ev += [("logit_max", g6)]
        if g8 is not None:
            ev += [("wT", g8)]
        put(t + 2, "zK", t + 2)
        put(t + 6, "down", t + 6)
        put(t + 1, "score", t + 1, 3)
        put(t, "prob", t, 3)
        put(t, "low", t, 2)
        put(t + 2, "yQ", t + 2)
        if g8 is not None:
            ev += [("pool", g8)]
        put(t + 1, "score", t + 1, 4)
        put(t, "prob", t, 4)
        put(t, "low", t, 3)
        put(t + 2, "zV", t + 2)
        if (t + 3) % GB == 0 and on(t + 3):
            g = (t + 3) // GB
            ev += [("tok", g), ("centred", g)]
        put(t + 1, "minus_max", t + 1)
        put(t, "low", t, 4)
        if (t + 3) % GB == 0 and on(t + 3):
            ev += [("split_z", g)]
            if g + 2 < G:
                ev += [("gn_mean", g + 2), ("gn_var", g + 2), ("normalise", g + 2)]
    ev += [("hidden", 0), ("experts", 0), ("turned", 0)] + [("scatter", g) for g in range(G)]
    return ev


EVENTS = schedule()
ON_A = ("xT", "small", "dnT", "gn_mean", "gn_var", "proj", "score", "uT", "shift", "down", "wT", "pool", "centred", "yQ",
        "experts", "turned", "scatter")
ON_B = ("up", "prob", "logits", "pv", "tok", "zK", "zV", "hidden")
A = {e: n for n, e in enumerate(e for e in EVENTS if e[0] in ON_A)}
BU = {e: n for n, e in enumerate(e for e in EVENTS if e[0] in ON_B)}


def hybrid_kernel(nc, x, bias, up_filter, dn_filter, Wq, Wk, Wv, gate_w, gate_b, weight1, weight2, out):
    def by_token(v):
        return v.rearrange("b h w c -> b (h w) c").rearrange("(g b) (a p r) c -> g p b a (r c)", g=G, a=2, r=R)

    x_tokens, out_tokens = by_token(x), by_token(out)
    cst_dram = nc.inline_tensor(constants(), name="shape_constants").ap()
    tables = nc.dram_tensor("filter_tables", (2, AROWS, TROW), F32, kind="Internal").ap()

    with ExitStack() as ctx:
        def sb(name, shape, dt=F32):
            return ctx.enter_context(nc.sbuf_tensor(name, shape, dt))

        def sem(name):
            return ctx.enter_context(nc.semaphore(name))

        cst = sb("cst", [P, C_COLS])
        ident = cst[:, C_ID:C_ID + P]
        ident_b = sb("ident_b", [P, P], BF16)
        mask_b = sb("mask_b", [P, P], BF16)
        ident_h = sb("ident_h", [P, P], F16)
        x_all = sb("x_all", [P, G, SLOT])
        xF_all = sb("xF_all", [P, G, SLOT])
        xin = sb("xin", [P, 2, SLOT])
        biasr = sb("biasr", [P, H])
        stats = sb("stats", [P, 6])
        mv = sb("mv", [P, G, GB, 2])
        gmean = sb("gmean", [P, G, GB])
        gvar = sb("gvar", [P, G, GB])
        grstd = sb("grstd", [P, G, GB])
        gdiff = sb("gdiff", [P, GB])
        pads = sb("pads", [32, 2, TROW])
        dnrow = sb("dnrow", [32, TAPS])
        UU = sb("UU", [P, SPAN, 2, 2 * W])
        D = sb("D", [P, NS, C])
        DD = sb("DD", [P, SPAN, R, C])
        y = sb("y", [P, 2, R, BC])
        tF = sb("tF", [P, SLOT])
        sq_z = sb("sq_z", [P, SLOT])
        zss = sb("zss", [P, 32])
        zrstd = sb("zrstd", [P, 32])
        z32 = sb("z32", [P, 32, C])
        z4 = sb("z4", [P, 32, 4, C], F16)
        zK = sb("zK", [P, 3, S], F16)
        yQ = sb("yQ", [P, 3, S], F16)
        zV = sb("zV", [P, 3, KT, 2 * C], F16)
        negmax = sb("negmax", [P, 2, KT])
        M4 = sb("M4", [P, KT, 4, C], F16)
        e32 = sb("e32", [P, 2, SLOT])
        Pp = sb("Pp", [P, 2, 2, PCOLS], F16)
        oT = sb("oT", [P, 2, S])
        t2_all = sb("t2_all", [P, G, SLOT])
        uT = sb("uT", [P, S])
        att = uT
        rsum = sb("rsum", [P, 2, KT, 2])
        nmean = sb("nmean", [P, 32])
        uss = sb("uss", [P, 32])
        urstd = sb("urstd", [P, 32])
        sq_u = sb("sq_u", [P, SLOT])
        u = sb("u", [P, KT, P])
        lg = sb("lg", [GE, S])
        probs = sb("probs", [GE, S])
        rest = sb("rest", [GE, S])
        top8 = sb("top8", [GE, TOP])
        ntop = sb("ntop", [GE, 1])
        esum = sb("esum", [GE, 1])
        wT = sb("wT", [P, KT, GE])
        pooled = sb("pooled", [C + 1, E_, B])
        wq_sb = sb("wq_sb", [C, C])
        wk_sb = sb("wk_sb", [C, C])
        wv_sb = sb("wv_sb", [C, C])
        gw_sb = sb("gw_sb", [E_, GB, C])
        gb_sb = sb("gb_sb", [GE, 1])
        wvT = sb("wvT", [C, C])
        A_sb = sb("A_sb", [C, C])
        T1 = sb("T1", [C, R, C])
        gateT = sb("gateT", [P, GB, E_])
        V2 = sb("V2", [P, 2 * C + 2])
        Bs = sb("Bs", [P, C])
        BB = sb("BB", [P, 4, C], F16)
        ones = sb("ones", [1, B])
        power = sb("power", [P, 1])
        hid = sb("hid", [HID, E_, B])
        o2 = sb("o2", [C, B, E_])
        obd = sb("obd", [GE, G, GB, C])
        early = Pp[:, :, :, :].rearrange("p i j n -> p (i j n)").bitcast(F32)

        def early_part(rows, at, n, a):
            return early[0:rows, at:at + a * n].rearrange("p (a t) -> p a t", a=a)

        upE = early_part(P, 0, EW, AROWS)
        upD = early_part(P, 1024, 2 * W, AROWS)
        dnE = early_part(C, 2048, 2 * W, AROWS)
        U = early[:, 3072:3072 + NS * P].rearrange("p (m q t) -> p m q t", m=NS, q=2)
        yflat = y[:, :, :, :].rearrange("p i t n -> p (i t n)")
        w1_sb = yflat[0:C + 1].rearrange("p (e h) -> p e h", e=E_)
        w2_sb = xin[:, 0, 0:E_ * C].rearrange("p (e c) -> p e c", e=E_)
        w2b_sb = xin[0:1, 1, 0:E_ * C].rearrange("p (e c) -> p e c", e=E_)

        psA = ctx.enter_context(nc.psum_tensor("psA", [P, 2, SLOT], F32))
        psB = ctx.enter_context(nc.psum_tensor("psB", [P, 2, SLOT], F32))

        def slot(e):
            return psA[:, A[e] % 2, :] if e in A else psB[:, BU[e] % 2, :]

        x_loaded = [sem(f"x_loaded{g}") for g in range(G)]
        cst_loaded = sem("cst_loaded")
        proj_loaded = sem("proj_loaded")
        ffn_loaded = sem("ffn_loaded")
        filters_loaded = sem("filters_loaded")
        dn_reversed = sem("dn_reversed")
        tables_stored = sem("tables_stored")
        toeplitz_loaded = sem("toeplitz_loaded")
        pads_zero = sem("pads_zero")
        fills_ready = sem("fills_ready")
        power_ready = sem("power_ready")
        masks_ready = sem("masks_ready")
        a_filled, a_drained = sem("a_filled"), sem("a_drained")
        b_filled, b_drained = sem("b_filled"), sem("b_drained")
        U_ready = sem("U_ready")
        UU_ready = sem("UU_ready")
        DD_ready = sem("DD_ready")
        stats_ready = sem("stats_ready")
        g_rstd = sem("g_rstd")
        xn_ready = sem("xn_ready")
        xin_ready = sem("xin_ready")
        y_ready = sem("y_ready")
        z_squared = sem("z_squared")
        z_var, z_rstd = sem("z_var"), sem("z_rstd")
        z_split = sem("z_split")
        z4_ready = sem("z4_ready")
        y_high = sem("y_high")
        max_ready = sem("max_ready")
        low_ready = sem("low_ready")
        t2_mean = sem("t2_mean")
        t2_centred = sem("t2_centred")
        t2_squared = sem("t2_squared")
        t2_var = sem("t2_var")
        t2_rstd = sem("t2_rstd")
        u_ready = sem("u_ready")
        lg_max = sem("lg_max")
        lg_exp = sem("lg_exp")
        route_ready = sem("route_ready")
        result = sem("result")
        stored = sem("stored")
        dve_chain = sem("dve_chain")

        block = ctx.enter_context(nc.Block())

        @block.sync
        def _(sp):
            sp.dma_start(x_all[:, 0, :].rearrange("p (b a n) -> p b a n", b=GB, a=2), x_tokens[0]).then_inc(x_loaded[0], 16)
            sp.dma_start(cst[:, :], cst_dram).then_inc(cst_loaded, 16)
            sp.dma_start(wq_sb[:, :], Wq).then_inc(proj_loaded, 16)
            sp.dma_start(wk_sb[:, :], Wk).then_inc(proj_loaded, 16)
            sp.dma_start(wv_sb[:, :], Wv).then_inc(proj_loaded, 16)
            for b in range(GB):
                sp.dma_start(gw_sb[:, b, :], gate_w).then_inc(proj_loaded, 16)
            for g in range(1, G):
                sp.dma_start(x_all[:, g, :].rearrange("p (b a n) -> p b a n", b=GB, a=2), x_tokens[g]).then_inc(x_loaded[g], 16)
            for b in range(GB):
                sp.dma_start(gb_sb[E_ * b:E_ * b + E_, :], gate_b.rearrange("(e a) -> e a", a=1)).then_inc(proj_loaded, 16)
            sp.wait_ge(a_filled, A["down", B - 1] + 1)
            sp.dma_start(w1_sb, weight1.rearrange("e d h -> d e h")).then_inc(ffn_loaded, 16)
            sp.dma_start(w2_sb, weight2[:, 0:HID, :].rearrange("e h o -> h e o")).then_inc(ffn_loaded, 16)
            sp.dma_start(w2b_sb, weight2[:, HID:HID + 1, :].rearrange("e h o -> h e o")).then_inc(ffn_loaded, 16)
            for g in range(G):
                sp.wait_ge(result, g + 1)
                sp.dma_start(out_tokens[g], x_all[:, g, :].rearrange("p (b a n) -> p b a n", b=GB, a=2)).then_inc(stored, 16)
            sp.wait_ge(stored, 16 * G)

        @block.gpsimd
        def _(pool):
            nc.gpsimd.memset(pads[:, :, :], 0.0).then_inc(pads_zero, 1)
            nc.gpsimd.memset(dnrow[:, :], 0.0).then_inc(pads_zero, 1)
            nc.gpsimd.memset(power[:, :], -0.5).then_inc(power_ready, 1)
            nc.gpsimd.memset(UU[:, :, :, :], 0.0).then_inc(fills_ready, 1)
            nc.gpsimd.memset(DD[:, :, :, :], 0.0).then_inc(fills_ready, 1)
            nc.gpsimd.memset(z32[:, :, :], 1.0).then_inc(fills_ready, 1)
            nc.gpsimd.memset(M4[:, :, :, :], 0.0).then_inc(fills_ready, 1)
            nc.gpsimd.memset(pooled[:, :, :], 1.0).then_inc(fills_ready, 1)
            nc.gpsimd.memset(ones[:, :], 1.0).then_inc(fills_ready, 1)
            pool.wait_ge(power_ready, 1)

            def inverse_root(v, n):
                return nc.gpsimd.tensor_tensor(v, v, power[:, 0:1].broadcast_to([P, n]), ALU.pow)

            def image_input(g):
                pool.wait_ge(xn_ready, g + 1)
                if g == 0:
                    pool.wait_ge(filters_loaded, 48)
                if g >= 2:
                    pool.wait_ge(b_filled, BU["up", GB * (g - 1) - 1] + 1)
                nc.gpsimd.tensor_tensor(xin[:, g % 2, :].rearrange("p (b h j) -> p b h j", b=GB, h=H),
                                        x_all[:, g, :].rearrange("p (b h j) -> p b h j", b=GB, h=H),
                                        biasr[:, :].unsqueeze(1).unsqueeze(3).broadcast_to([P, GB, H, JW]),
                                        ALU.add).then_inc(xin_ready, 1)

            for e in EVENTS:
                name, g = e[0], e[1]
                if name == "gn_var":
                    pool.wait_ge(a_drained, A["gn_var", g] + 1)
                    inverse_root(grstd[:, g, :], GB).then_inc(g_rstd, 1)
                elif name == "normalise":
                    image_input(g)
                elif name == "centred":
                    pool.wait_ge(z_var, g + 1)
                    inverse_root(zrstd[:, :], 32).then_inc(z_rstd, 1)
                elif name == "split_z":
                    pool.wait_ge(z_split, g + 1)
                    nc.gpsimd.tensor_copy(z4[:, :, 2:4, :], z4[:, :, 0:2, :]).then_inc(z4_ready, 1)
                elif name == "mean":
                    pool.wait_ge(t2_mean, g + 1)
                    if g >= 1:
                        pool.wait_ge(a_filled, A["pool", g - 1] + 1)
                    nc.gpsimd.tensor_tensor(u[:, :, :].rearrange("p k (b c) -> p b k c", b=GB),
                                            t2_all[:, g, :].rearrange("p (b k c) -> p b k c", b=GB, k=KT),
                                            nmean[:, :].rearrange("p (b k) -> p b k", b=GB).unsqueeze(3).broadcast_to([P, GB, KT, C]),
                                            ALU.add).then_inc(t2_centred, 1)
                elif name == "dev":
                    v = u[:, :, :].rearrange("p k (b c) -> p (k b) c", c=C)
                    pool.wait_ge(t2_var, g + 1)
                    inverse_root(urstd[:, :], 32).then_inc(t2_rstd, 1)
                    pool.wait_ge(t2_rstd, g + 1)
                    nc.gpsimd.tensor_tensor(v, v, urstd[:, :].unsqueeze(2).broadcast_to([P, 32, C]), ALU.mult).then_inc(u_ready, 1)

        @block.scalar
        def _(act):
            act.wait_ge(pads_zero, 2)
            act.dma_start(pads[2:2 + TAPS, 0, UP_AT:UP_AT + TAPS], up_filter[0, 0]).then_inc(filters_loaded, 16)
            act.dma_start(dnrow[2:2 + TAPS, :], dn_filter[0, 0]).then_inc(filters_loaded, 16)
            act.dma_start(biasr[:, :], bias.rearrange("a h c d -> a (h c d)").broadcast_to([P, H])).then_inc(filters_loaded, 16)
            act.wait_ge(filters_loaded, 48)
            act.wait_ge(dn_reversed, 1)
            act.dma_start(tables.rearrange("f a t -> a f t"), pads[0:AROWS, :, :]).then_inc(tables_stored, 16)
            act.wait_ge(tables_stored, 16)
            up_src = bass.AP(tensor=tables.tensor, offset=0, ap=[[2, C], [TROW, AROWS], [1, EW]])
            dn_src = bass.AP(tensor=tables.tensor, offset=AROWS * TROW, ap=[[2, C], [TROW, AROWS], [1, 2 * W]])
            for b in range(R):
                act.dma_start(upE[C * b:C * b + C, :, :], up_src).then_inc(toeplitz_loaded, 16)
            act.dma_start(dnE[:, :, :], dn_src).then_inc(toeplitz_loaded, 16)

            for e in EVENTS:
                name, n = e[0], e[1]
                if e in BU:
                    act.wait_ge(b_filled, BU[e] + 1)
                if name == "up":
                    if n >= 2:
                        act.wait_ge(a_filled, A["down", n - 2] + 1)
                    nc.scalar.activation(y[:, n % 2, :, :].rearrange("p t n -> p (t n)"), slot(e), ACT.Copy).then_inc(b_drained, 1)
                elif name == "tok":
                    nc.scalar.activation(t2_all[:, n, :], slot(e), ACT.Copy).then_inc(b_drained, 1)
                elif name == "centred":
                    act.wait_ge(a_filled, A[e] + 1)
                    if n >= 1:
                        act.wait_ge(z_var, n)
                    nc.scalar.activation(sq_z[:, :], slot(e), ACT.Square).then_inc(z_squared, 1)
                elif name == "zK":
                    src = slot(e).bitcast(F16)[:, 0:S].rearrange("p (a r q) -> p a r q", a=2, r=R)
                    nc.scalar.activation(zK[:, n % 3, :].rearrange("p (a q r) -> p a r q", a=2, r=R), src,
                                         ACT.Copy).then_inc(b_drained, 1)
                elif name == "zV":
                    nc.scalar.activation(zV[:, n % 3, :, :].rearrange("p k d -> p (k d)"), slot(e).bitcast(F16)[:, 0:KT * 2 * C],
                                         ACT.Copy).then_inc(b_drained, 1)
                elif name == "yQ":
                    act.wait_ge(a_filled, A[e] + 1)
                    nc.scalar.activation(yQ[:, n % 3, :], slot(e), ACT.Copy).then_inc(y_high, 1)
                elif name == "prob":
                    m = NU * n + e[2]
                    if m >= 2:
                        act.wait_ge(low_ready, m - 1)
                    N = UCOLS[e[2]]
                    nc.scalar.activation(e32[:, m % 2, 0:N], slot(e)[:, 0:N], ACT.Exp)
                    nc.scalar.activation(Pp[:, n % 2, 0, UOFF[e[2]]:UOFF[e[2]] + N], slot(e)[:, 0:N], ACT.Exp).then_inc(b_drained, 1)
                elif name == "pv":
                    nc.scalar.activation(oT[64 * (n % 2):64 * (n % 2) + 64, n // 2 % 2, :], slot(e)[0:64, :],
                                         ACT.Copy).then_inc(b_drained, 1)
                elif name == "mean":
                    act.wait_ge(t2_centred, n + 1)
                    nc.scalar.activation(sq_u[:, :], u[:, :, :].rearrange("p k d -> p (k d)"), ACT.Square).then_inc(t2_squared, 1)
                elif name == "logits":
                    nc.scalar.activation(lg[:, :], slot(e)[0:GE, :], ACT.Identity, bias=gb_sb[:, 0:1]).then_inc(b_drained, 1)
                elif name == "logit_exp":
                    act.wait_ge(lg_max, n + 1)
                    nc.scalar.activation(probs[:, :], lg[:, :], ACT.Exp, bias=ntop[:, 0:1],
                                         accum_out=esum[:, 0:1]).then_inc(lg_exp, 1)
                elif name == "hidden":
                    nc.scalar.activation(hid[:, :, :], slot(e)[:, 0:E_ * B].rearrange("p (e b) -> p e b", e=E_),
                                         ACT.Gelu).then_inc(b_drained, 1)

        @block.vector
        def _(dve):
            chained = [0]

            def link(ins):
                chained[0] += 1
                ins.then_inc(dve_chain, 1)
                dve.wait_ge(dve_chain, chained[0])

            def blocks(n, m, like, first=C_BD):
                return cst[0:like, first:first + n].unsqueeze(2).broadcast_to([like, n, m])

            dve.wait_ge(filters_loaded, 48)
            nc.vector.tensor_copy(pads[:, 1, DN_AT:DN_AT + TAPS], dnrow[:, ::-1]).then_inc(dn_reversed, 1)
            dve.wait_ge(cst_loaded, 16)
            nc.vector.tensor_copy(ident_b[:, :], ident).then_inc(masks_ready, 1)
            nc.vector.tensor_copy(mask_b[:, :], cst[:, C_MASK:C_MASK + P]).then_inc(masks_ready, 1)
            nc.vector.tensor_copy(ident_h[:, :], ident).then_inc(masks_ready, 1)

            for e in EVENTS:
                name, n = e[0], e[1]
                if e in A and name not in ("centred", "yQ"):
                    dve.wait_ge(a_filled, A[e] + 1)
                s = slot(e) if e in A else None
                if name == "xT":
                    nc.vector.tensor_copy(xF_all[:, n, :], s).then_inc(a_drained, 1)
                    dve.wait_ge(a_drained, A[e] + 1)
                    for b in range(GB):
                        link(nc.vector.bn_stats(stats[:, :], xF_all[:, n, BC * b:BC * b + BC]))
                        ins = nc.vector.bn_aggr(mv[:, n, b, :], stats[:, :])
                        if b < GB - 1:
                            link(ins)
                    ins.then_inc(stats_ready, 1)
                elif name == "gn_mean":
                    link(nc.vector.tensor_copy(gmean[:, n, :], s[:, 0:GB]))
                    link(nc.vector.tensor_tensor(gdiff[:, :], mv[:, n, :, 0], gmean[:, n, :], ALU.subtract))
                    link(nc.vector.tensor_tensor(gdiff[:, :], gdiff[:, :], gdiff[:, :], ALU.mult))
                    nc.vector.tensor_tensor(gvar[:, n, :], mv[:, n, :, 1], gdiff[:, :], ALU.add).then_inc(a_drained, 1)
                elif name == "gn_var":
                    nc.vector.tensor_scalar(grstd[:, n, :], s[:, 0:GB], EPS, None, ALU.add).then_inc(a_drained, 1)
                elif name == "normalise":
                    dve.wait_ge(g_rstd, n + 1)
                    for b in range(GB):
                        r = slice(BC * b, BC * b + BC)
                        ins = nc.vector.tensor_scalar(x_all[:, n, r], xF_all[:, n, r], gmean[:, n, b:b + 1], grstd[:, n, b:b + 1],
                                                      ALU.subtract, ALU.mult)
                    ins.then_inc(xn_ready, 1)
                    if n == 0:
                        dve.wait_ge(toeplitz_loaded, 16 * 5)
                        link(nc.vector.tensor_tensor(upD, upE[:, :, 0:2 * W], upE[:, :, 1:2 * W + 1], ALU.add))
                        nc.vector.tensor_tensor(U[:, :, 0, :], upD[:, 1:2 * NS:2, :], upD[:, 2:2 * NS + 1:2, :], ALU.add).then_inc(U_ready, 1)
                        nc.vector.tensor_tensor(U[:, :, 1, :], upD[:, 0:2 * NS - 1:2, :], upD[:, 1:2 * NS:2, :], ALU.add).then_inc(U_ready, 1)
                        dve.wait_ge(U_ready, 2)
                        dve.wait_ge(fills_ready, 6)
                        for r in range(R):
                            q = slice(C * r, C * r + C)
                            nc.vector.tensor_copy(UU[q, R - 1 - r:R - 1 - r + NS, :, :], U[q, :, :, :]).then_inc(UU_ready, 1)
                elif name == "small" and n == 0:
                    link(nc.vector.tensor_copy(wvT[:, :], s[0:C, 0:C]))
                    link(nc.vector.tensor_copy(A_sb[:, :], s[0:C, P:P + C]))
                    nc.vector.tensor_tensor(gateT[:, :, :], s[:, BANK:BANK + E_].unsqueeze(1).broadcast_to([P, GB, E_]),
                                            blocks(GB, E_, P), ALU.mult).then_inc(a_drained, 1)
                elif name == "small" and n == 1:
                    link(nc.vector.tensor_copy(T1[:, :, :], s[0:C, 0:C].unsqueeze(1).broadcast_to([C, R, C])))
                    link(nc.vector.tensor_copy(V2[:, 2 * C:2 * C + 2], cst[:, C_SUM:C_SUM + 2]))
                    nc.vector.tensor_tensor(V2[:, 0:2 * C].rearrange("p (b c) -> p b c", b=2), s[:, BANK:BANK + C].unsqueeze(1).broadcast_to([P, 2, C]),
                                            blocks(2, C, P, C_HALF), ALU.mult).then_inc(a_drained, 1)
                elif name == "small":
                    link(nc.vector.tensor_scalar(Bs[:, :], s[:, 0:C], float(C) ** -0.5, None, ALU.mult))
                    link(nc.vector.tensor_copy(BB[:, :, :], Bs[:, :].unsqueeze(1).broadcast_to([P, 4, C])))
                    nc.vector.tensor_tensor(BB[2 * C:P, :, :], Bs[2 * C:P, :].unsqueeze(1).broadcast_to([2 * C, 4, C]),
                                            BB[2 * C:P, :, :], ALU.subtract).then_inc(a_drained, 1)
                elif name == "dnT":
                    link(nc.vector.tensor_copy(D[:, :, :], s[:, 0:NS * C].rearrange("p (m c) -> p m c", m=NS)))
                    for r in range(R):
                        ins = nc.vector.tensor_copy(DD[:, r:r + NS, r, :], D[:, :, :])
                    ins.then_inc(a_drained, 1)
                elif name == "leak":
                    v = y[:, n % 2, :, :].rearrange("p t n -> p (t n)")
                    dve.wait_ge(b_drained, BU["up", n] + 1)
                    nc.vector.scalar_tensor_tensor(out=v, in0=v, scalar=SLOPE, in1=v, op0=ALU.mult, op1=ALU.max).then_inc(y_ready, 1)
                elif name == "down":
                    b = n % GB
                    nc.vector.scalar_tensor_tensor(out=tF[:, BC * b:BC * b + BC], in0=s[:, 0:BC], scalar=GAIN,
                                                   in1=xF_all[:, n // GB, BC * b:BC * b + BC], op0=ALU.mult, op1=ALU.add).then_inc(a_drained, 1)
                elif name == "centred":
                    dve.wait_ge(z_squared, n + 1)
                    link(nc.vector.tensor_reduce(zss[:, :], sq_z[:, :].rearrange("p (n c) -> p n c", c=C), X, ALU.add))
                    nc.vector.tensor_scalar(zrstd[:, :], zss[:, :], 1.0 / C, EPS, ALU.mult, ALU.add).then_inc(z_var, 1)
                elif name == "split_z":
                    s = slot(("centred", n)).rearrange("p (n c) -> p n c", c=C)
                    dve.wait_ge(z_rstd, n + 1)
                    if n >= 1:
                        dve.wait_ge(b_filled, BU["zK", GB * n - 1] + 1)
                    nc.vector.tensor_tensor(z32[:, :, 0:C - 1], s[:, :, 0:C - 1],
                                            zrstd[:, :].unsqueeze(2).broadcast_to([P, 32, C - 1]), ALU.mult).then_inc(a_drained, 1)
                    dve.wait_ge(a_drained, A["centred", n] + 1)
                    link(nc.vector.tensor_copy(z4[:, :, 0, :], z32[:, :, :]))
                    nc.vector.tensor_tensor(z4[:, :, 1, :], z32[:, :, :], z4[:, :, 0, :], ALU.subtract).then_inc(z_split, 1)
                elif name == "yQ":
                    dve.wait_ge(y_high, n + 1)
                    v = yQ[2 * C:P, n % 3, :]
                    nc.vector.tensor_tensor(v, s[2 * C:P, :], v, ALU.subtract).then_inc(a_drained, 1)
                elif name == "score":
                    for k, (m, at) in enumerate(packed(e[2])):
                        ins = nc.vector.tensor_reduce(negmax[:, n % 2, m - 1:m], s[:, at:at + P * m], X, ALU.max, negate=True)
                    ins.then_inc(a_drained, 1)
                elif name == "minus_max":
                    dve.wait_ge(a_drained, A["score", n, NU - 1] + 1)
                    v = negmax[:, n % 2, :].unsqueeze(2).broadcast_to([P, KT, 2])
                    link(nc.vector.tensor_copy(M4[:, :, 0:2, C - 1], v))
                    nc.vector.tensor_tensor(M4[:, :, 2:4, C - 1], v, M4[:, :, 0:2, C - 1], ALU.subtract).then_inc(max_ready, 1)
                elif name == "shift":
                    v = yQ[:, n % 3, :]
                    nc.vector.tensor_tensor(v, v, s.bitcast(F16)[:, 0:S], ALU.add).then_inc(a_drained, 1)
                elif name == "low":
                    m, N, o = NU * n + e[2], UCOLS[e[2]], UOFF[e[2]]
                    dve.wait_ge(b_drained, BU["prob", n, e[2]] + 1)
                    nc.vector.tensor_tensor(Pp[:, n % 2, 1, o:o + N], e32[:, m % 2, 0:N], Pp[:, n % 2, 0, o:o + N],
                                            ALU.subtract).then_inc(low_ready, 1)
                elif name == "proj":
                    sv = s.rearrange("p (k d) -> p k d", k=KT)
                    av = att[:, :].rearrange("p (b k c) -> p k b c", b=GB, k=KT)[:, :, 2 * e[2]:2 * e[2] + 2, :]
                    link(nc.vector.reciprocal(rsum[:, e[2], :, :], sv[:, :, 2 * C:2 * C + 2]))
                    nc.vector.tensor_tensor(av, sv[:, :, 0:2 * C].rearrange("p k (b c) -> p k b c", b=2),
                                            rsum[:, e[2], :, :].unsqueeze(3).broadcast_to([P, KT, 2, C]), ALU.mult).then_inc(a_drained, 1)
                elif name == "mean":
                    dve.wait_ge(a_drained, A["proj", n, 1] + 1)
                    dve.wait_ge(b_drained, BU["tok", n] + 1)
                    link(nc.vector.tensor_tensor(t2_all[:, n, :], t2_all[:, n, :], att[:, :], ALU.add))
                    link(nc.vector.tensor_reduce(nmean[:, :], t2_all[:, n, :].rearrange("p (n c) -> p n c", c=C), X, ALU.add))
                    nc.vector.tensor_scalar(nmean[:, :], nmean[:, :], -1.0 / C, None, ALU.mult).then_inc(t2_mean, 1)
                elif name == "dev":
                    dve.wait_ge(t2_squared, n + 1)
                    link(nc.vector.tensor_reduce(uss[:, :], sq_u[:, :].rearrange("p (n c) -> p n c", c=C), X, ALU.add))
                    nc.vector.tensor_scalar(urstd[:, :], uss[:, :], 1.0 / C, EPS, ALU.mult, ALU.add).then_inc(t2_var, 1)
                elif name == "uT":
                    nc.vector.tensor_copy(uT[:, :].rearrange("p (a q r) -> p a r q", a=2, r=R),
                                          s.rearrange("p (a r q) -> p a r q", a=2, r=R)).then_inc(a_drained, 1)
                elif name == "logit_max":
                    dve.wait_ge(b_drained, BU["logits", n] + 1)
                    link(nc.vector.max(top8[:, :], lg[:, :]))
                    nc.vector.tensor_scalar(ntop[:, :], top8[:, 0:1], -1.0, None, ALU.mult).then_inc(lg_max, 1)
                elif name == "route":
                    dve.wait_ge(lg_exp, n + 1)
                    link(nc.vector.reciprocal(esum[:, :], esum[:, :]))
                    link(nc.vector.tensor_scalar(probs[:, :], probs[:, :], esum[:, 0:1], None, ALU.mult))
                    link(nc.vector.max(top8[:, :], probs[:, :]))
                    link(nc.vector.match_replace(rest[:, :], top8[:, :], probs[:, :], 0.0))
                    nc.vector.tensor_tensor(xF_all[0:GE, n, :], probs[:, :], rest[:, :], ALU.subtract).then_inc(route_ready, 1)
                elif name == "wT":
                    nc.vector.tensor_copy(wT[:, :, :].rearrange("p k n -> p (k n)"), s[:, 0:KT * GE]).then_inc(a_drained, 1)
                elif name == "pool":
                    for b in range(GB):
                        ins = nc.vector.tensor_copy(pooled[0:C, :, GB * n + b], s[C * b:C * b + C, E_ * b:E_ * b + E_])
                    ins.then_inc(a_drained, 1)
                elif name == "experts":
                    nc.vector.tensor_copy(o2[:, :, :], s[0:C, 0:B * E_].rearrange("p (b e) -> p b e", b=B)).then_inc(a_drained, 1)
                elif name == "turned":
                    for g in range(G):
                        ins = nc.vector.tensor_tensor(obd[:, g, :, :], s[0:GE, C * g:C * g + C].unsqueeze(1).broadcast_to([GE, GB, C]),
                                                      blocks(GB, C, GE, C_BDE), ALU.mult)
                    ins.then_inc(a_drained, 1)
                elif name == "scatter":
                    nc.vector.tensor_tensor(x_all[:, n, :].rearrange("p (b k c) -> p k b c", b=GB, k=KT),
                                            s.rearrange("p (k b c) -> p k b c", b=GB, k=KT),
                                            t2_all[:, n, :].rearrange("p (b k c) -> p k b c", b=GB, k=KT), ALU.add).then_inc(result, 1)

        @block.tensor
        def _(pe):
            def by_tile(v):
                w = v.rearrange("p (a q r) -> p a r q", a=2, r=R)
                return lambda k: w[:, k // R, k % R, :]

            def turn(s, src, idn, n=P):
                for k in range(KT):
                    ins = nc.tensor.transpose(s[:, n * k:n * k + n], src(k), idn)
                return ins

            def within(v, shift):
                return v.rearrange("p (h j) -> p h j", j=JW)[:, :, max(0, shift):JW + min(0, shift)]

            def convolve(out_cols, matrices):
                for i, (m, v, shift) in enumerate(sorted(matrices, key=lambda a: a[2] != 0)):
                    ins = nc.tensor.matmul(within(out_cols, -shift), m, within(v, shift), start=i == 0, stop=i == len(matrices) - 1)
                return ins

            def pieces(first, last):
                cuts = [first] + [c for c in (BANK,) if first < c < last] + [last]
                return list(zip(cuts, cuts[1:]))

            pe.wait_ge(cst_loaded, 16)
            for e in EVENTS:
                name, n = e[0], e[1]
                if e in A:
                    if name == "scatter" and n >= 2:
                        pe.wait_ge(result, n - 1)
                    elif A[e] >= 2:
                        pe.wait_ge(a_drained, A[e] - 1)
                if e in BU and BU[e] >= 2:
                    pe.wait_ge(b_drained, BU[e] - 1)
                s = slot(e) if e in A or e in BU else None
                if name == "xT":
                    pe.wait_ge(x_loaded[n], 16)
                    ins = turn(s, lambda k: x_all[:, n, P * k:P * k + P], ident)
                elif name == "gn_mean":
                    pe.wait_ge(stats_ready, n + 1)
                    ins = nc.tensor.matmul(s[:, 0:GB], cst[:, C_AVG:C_AVG + P], mv[:, n, :, 0], start=True, stop=True)
                elif name == "gn_var":
                    pe.wait_ge(a_drained, A["gn_mean", n] + 1)
                    ins = nc.tensor.matmul(s[:, 0:GB], cst[:, C_AVG:C_AVG + P], gvar[:, n, :], start=True, stop=True)
                elif name == "small" and n == 0:
                    pe.wait_ge(proj_loaded, 16 * 11)
                    nc.tensor.matmul(s[0:C, 0:C], wv_sb[:, :], ident[0:C, 0:C], start=True, stop=True)
                    nc.tensor.matmul(s[0:C, P:P + C], wq_sb[:, :], wk_sb[:, :], start=True, stop=True)
                    ins = nc.tensor.matmul(s[:, BANK:BANK + E_], gw_sb[:, :, :], ident[0:E_, 0:E_], start=True, stop=True)
                elif name == "small" and n == 1:
                    pe.wait_ge(a_drained, A["small", 0] + 1)
                    nc.tensor.matmul(s[0:C, 0:C], A_sb[:, :], cst[0:C, C_Q:C_Q + C], start=True, stop=True)
                    ins = nc.tensor.matmul(s[:, BANK:BANK + C], cst[0:C, C_QREP:C_QREP + P], wvT[:, :], start=True, stop=True)
                elif name == "small":
                    pe.wait_ge(a_drained, A["small", 1] + 1)
                    ins = nc.tensor.matmul(s[:, 0:C], T1[:, :, :], cst[0:C, C_Q:C_Q + C], start=True, stop=True)
                elif name == "dnT":
                    pe.wait_ge(toeplitz_loaded, 16 * 5)
                    rows = dnE.rearrange("p a t -> p (a t)")
                    for m in range(NS):
                        ins = nc.tensor.matmul(s[:, C * m:C * m + C], rows[:, 2 * W * (2 * m + 1):2 * W * (2 * m + 3)], ident[0:C, 0:C],
                                               start=True, stop=True)
                elif name == "up":
                    if n % GB == 0:
                        pe.wait_ge(xin_ready, n // GB + 1)
                    if n == 0:
                        pe.wait_ge(UU_ready, R)
                    img = xin[:, n // GB % 2, BC * (n % GB):BC * (n % GB) + BC]
                    for t in range(R):
                        ins = convolve(s[:, BC * t:BC * t + BC],
                                       [(UU[:, R * k - t + NS - 1, :, :], img, k) for k in (-1, 0, 1) if 0 <= R * k - t + NS - 1 < SPAN])
                elif name == "down":
                    pe.wait_ge(y_ready, n + 1)
                    if n == 0:
                        pe.wait_ge(a_drained, A["dnT", 0] + 1)
                    ins = convolve(s[:, 0:BC], [(DD[:, R * k + t + 3, :, :], y[:, n % 2, t, :], k) for k in (-1, 0, 1)
                                                for t in range(R) if 0 <= R * k + t + 3 < SPAN])
                elif name == "tok":
                    pe.wait_ge(a_drained, A["down", GB * n + GB - 1] + 1)
                    ins = turn(s, lambda k: tF[:, P * k:P * k + P], ident)
                elif name == "centred":
                    for k in range(KT):
                        ins = nc.tensor.matmul(s[:, P * k:P * k + P], tF[:, P * k:P * k + P], cst[:, C_Q:C_Q + P], start=True, stop=True)
                elif name == "zK":
                    pe.wait_ge(z4_ready, n // GB + 1)
                    if n == 0:
                        pe.wait_ge(masks_ready, 3)
                    ins = turn(s.bitcast(F16), lambda k: z4[:, KT * (n % GB) + k, :, :], ident_h[:, :])
                elif name == "zV":
                    ins = turn(s.bitcast(F16), lambda k: zK[0:2 * C, n % 3, P * k:P * k + P], ident_h[0:2 * C, 0:2 * C], 2 * C)
                elif name == "yQ":
                    pe.wait_ge(b_drained, BU["zK", n] + 1)
                    if n == 0:
                        pe.wait_ge(a_drained, A["small", 2] + 1)
                    for i in range(2):
                        ins = nc.tensor.matmul(s[:, BANK * i:BANK * i + BANK], BB[:, :, :], zK[:, n % 3, BANK * i:BANK * i + BANK], start=True, stop=True)
                elif name == "score":
                    if e[2] == 0:
                        pe.wait_ge(a_drained, A["yQ", n] + 1)
                    for m, at in packed(e[2]):
                        for lo, hi in pieces(at, at + P * m):
                            diagonal = hi == at + P * m
                            ins = nc.tensor.matmul(s[:, lo:hi], yQ[:, n % 3, P * (m - 1):P * m], zK[:, n % 3, lo - at:hi - at],
                                                   start=True, stop=not diagonal)
                            if diagonal:
                                ins = nc.tensor.matmul(s[:, hi - P:hi], ident_b[:, :], mask_b[:, :], start=False, stop=True)
                elif name == "shift":
                    pe.wait_ge(max_ready, n + 1)
                    ins = turn(s.bitcast(F16), lambda k: M4[:, k, :, :], ident_h[:, :])
                elif name == "prob":
                    if e[2] == 0:
                        pe.wait_ge(a_drained, A["shift", n] + 1)
                    for m, at in packed(e[2]):
                        j = KT - m
                        for lo, hi in pieces(at, at + P * m):
                            diagonal = lo == at
                            ins = nc.tensor.matmul(s[:, lo:hi], zK[:, n % 3, P * j:P * j + P], yQ[:, n % 3, P * j + lo - at:P * j + hi - at],
                                                   start=True, stop=not diagonal)
                            if diagonal:
                                ins = nc.tensor.matmul(s[:, lo:lo + P], mask_b[:, :], ident_b[:, :], start=False, stop=True)
                elif name == "pv":
                    pe.wait_ge(low_ready, NU * (n + 1))
                    pe.wait_ge(b_drained, BU["zV", n] + 1)
                    for i in range(2):
                        last = R * (i + 1) - 1
                        for j in range(last + 1):
                            q = max(P * j, BANK * i)
                            N = BANK * (i + 1) - q
                            o = PLACE[j] + q - P * j
                            for part in range(2):
                                ins = nc.tensor.matmul(s[0:2 * C, q:q + N], zV[:, n % 3, j, :], Pp[:, n % 2, part, o:o + N],
                                                       start=j == 0 and part == 0, stop=j == last and part == 1)
                elif name == "proj":
                    pe.wait_ge(b_drained, BU["pv", GB * n + 2 * e[2] + 1] + 1)
                    tile = by_tile(oT[:, e[2], :])
                    for k in range(KT):
                        ins = nc.tensor.matmul(s[:, P * k:P * k + 2 * C + 2], tile(k), V2[:, :], start=True, stop=True)
                elif name == "uT":
                    pe.wait_ge(u_ready, n + 1)
                    ins = turn(s, lambda k: u[:, k, :], ident)
                elif name == "logits":
                    pe.wait_ge(a_drained, A["uT", n] + 1)
                    for i in range(2):
                        ins = nc.tensor.matmul(s[0:GE, BANK * i:BANK * i + BANK], gateT[:, :, :], uT[:, BANK * i:BANK * i + BANK], start=True, stop=True)
                elif name == "wT":
                    pe.wait_ge(route_ready, n + 1)
                    ins = turn(s, by_tile(xF_all[0:GE, n, :]), ident[0:GE, 0:GE], GE)
                elif name == "pool":
                    pe.wait_ge(a_drained, A["wT", n] + 1)
                    for k in range(KT):
                        ins = nc.tensor.matmul(s[:, 0:GE], u[:, k, :], wT[:, k, :], start=k == 0, stop=k == KT - 1)
                elif name == "hidden":
                    pe.wait_ge(ffn_loaded, 48)
                    pe.wait_ge(a_drained, A["pool", G - 1] + 1)
                    for x_ in range(E_):
                        ins = nc.tensor.matmul(s[:, B * x_:B * x_ + B], w1_sb[:, x_, :], pooled[:, x_, :], start=True, stop=True)
                elif name == "experts":
                    pe.wait_ge(b_drained, BU["hidden", 0] + 1)
                    sv = s[0:C, 0:B * E_].rearrange("p (b e) -> p e b", b=B)
                    for x_ in range(E_):
                        nc.tensor.matmul(sv[:, x_, :], w2_sb[:, x_, :], hid[:, x_, :], start=True, stop=False)
                        ins = nc.tensor.matmul(sv[:, x_, :], w2b_sb[:, x_, :], ones[:, :], start=False, stop=True)
                elif name == "turned":
                    pe.wait_ge(a_drained, A["experts", 0] + 1)
                    for g in range(G):
                        ins = nc.tensor.transpose(s[0:GE, C * g:C * g + C], o2[:, GB * g:GB * g + GB, :], ident[0:C, 0:C])
                elif name == "scatter":
                    pe.wait_ge(a_drained, A["turned", 0] + 1)
                    tile = by_tile(xF_all[0:GE, n, :])
                    for k in range(KT):
                        ins = nc.tensor.matmul(s[:, P * k:P * k + P], tile(k), obd[:, n, :, :], start=True, stop=True)
                else:
                    continue
                ins.then_inc(a_filled if e in A else b_filled, 1)


_INS = ['x', 'L0_conv_bias', 'L0_conv_up_filter', 'L0_conv_dn_filter', 'L1_attn_Wq', 'L1_attn_Wk', 'L1_attn_Wv',
        'L1_ffn_gate_w', 'L1_ffn_gate_b', 'L1_ffn_weight1', 'L1_ffn_weight2']
_OUTS = [((16, 32, 32, 32), 'float32')]


def kernel(**inputs):
    import numpy as _np
    import concourse.bacc as _bacc
    from concourse import mybir as _mybir
    from concourse.bass_utils import run_bass_kernel_spmd as _run

    nc = _bacc.Bacc("TRN2", target_bir_lowering=False, num_devices=1)
    arrays, args = {}, []
    for name in _INS:
        a = _np.ascontiguousarray(inputs[name])
        arrays[f"in_{name}_dram"] = a
        args.append(nc.dram_tensor(f"in_{name}_dram", a.shape, _mybir.dt.from_np(a.dtype), kind="ExternalInput").ap())
    for i, (shape, dtype) in enumerate(_OUTS):
        dt = _mybir.dt.from_np(_np.dtype(dtype))
        args.append(nc.dram_tensor(f"out_{i}_dram", shape, dt, kind="ExternalOutput").ap())
    hybrid_kernel(nc, *args)
    r = _run(nc, [arrays], core_ids=[0])
    return r.results[0]["out_0_dram"]
```

```python
from contextlib import ExitStack

import numpy as np

import concourse.bass as bass
from concourse import mybir

F32 = mybir.dt.float32
F16 = mybir.dt.float16
BF16 = mybir.dt.bfloat16
ALU = mybir.AluOpType
ACT = mybir.ActivationFunctionType
X = mybir.AxisListType.X

B, H, W, C = 16, 32, 32, 32
S = H * W
P = 128
R = P // C
JW = W // R
BC = H * JW
GB = 4
G = B // GB
KT = S // P
HB = KT // R
PIECES = ((0, BC), (BC, GB * BC))
TAPS = 12
NS = 7
SPAN = NS + R - 1
AROWS = 2 * NS + 1
TROW = 128
UP_AT, DN_AT = 58, 57
EW = 2 * W + 1
E_ = 16
HID = 128
GE = GB * E_
TOP = 8
LAST_PAIR = (G - 1, 1)
PARTS = ((0, B - GB), (B - GB, B))
POOL_LOW = (0, 2, 3)
SLOT = 1024
BANK = 512
NEG = -1.0e30
SLOPE, GAIN = 0.2, float(np.sqrt(2.0))
EPS = 1e-5
UP_SCALE = DOWN_SCALE = 64.0

PACK = [[8], [7, 1], [6, 2], [5, 3], [4]]
NU = len(PACK)


def packed(u):
    at, out = 0, []
    for n in PACK[u]:
        out.append((n, at))
        at += n * P
    return out


UCOLS = [sum(p) * P for p in PACK]
UOFF = [sum(UCOLS[:u]) for u in range(NU)]
PCOLS = sum(UCOLS)
PLACE = {KT - n: UOFF[u] + at for u in range(NU) for n, at in packed(u)}

C_ID, C_Q, C_QREP, C_MASK, C_AVG, C_BD, C_BDE, C_HALF, C_SUM, C_ROW, C_COLS = 0, 128, 256, 384, 512, 640, 644, 648, 650, 652, 653


def constants():
    q = np.zeros((C, C), np.float64)
    for i in range(C - 1):
        q[:i + 1, i] = 1.0 / np.sqrt((i + 1.0) * (i + 2.0))
        q[i + 1, i] = -(i + 1.0) / np.sqrt((i + 1.0) * (i + 2.0))
    t = np.zeros((P, C_COLS), np.float32)
    t[:, C_ID:C_ID + P] = np.eye(P)
    t[:, C_Q:C_Q + P] = np.kron(np.eye(R), q)
    t[:C, C_QREP:C_QREP + P] = np.tile(q, (1, R))
    t[:, C_MASK:C_MASK + P] = np.triu(np.full((P, P), NEG), 1)
    t[:, C_AVG:C_AVG + P] = np.tile(np.eye(C), (R, R)) / R
    t[:, C_BD:C_BD + GB] = np.kron(np.eye(GB), np.ones((C, 1)))
    t[:GE, C_BDE:C_BDE + GB] = np.kron(np.eye(GB), np.ones((E_, 1)))
    t[:, C_HALF:C_HALF + 2] = np.kron(np.eye(2), np.ones((2 * C, 1)))
    t[C - 1::C, C_SUM:C_SUM + 2] = np.kron(np.eye(2), np.ones((2, 1)))
    t[3 * C + 1, C_ROW] = -1.0
    return t


def batch(ahead, name, *more):
    return lambda t: (name, t + ahead) + more if 0 <= t + ahead < B else None


def group(late, name, *more):
    return lambda t: (name, (t - late) // GB) + more if (t - late) % GB == 0 and 0 <= t - late < B else None


def once(step, name, n):
    return lambda t: (name, n) if t == step else None


FIRST = [("xT", 0), ("gn_mean", 0), ("gn_var", 0), ("U", 0), ("normalise", 0), ("image", 0), ("UU", 0), ("image_low", 0)]
STEP = [batch(4, "up"), once(-3, "xT", 2), batch(2, "z_rstd"), batch(1, "score", 0), batch(0, "prob", 1),
        once(-1, "image", 1), group(7, "select"), group(5, "mean", 1), batch(-1, "low", 4), batch(1, "score", 2),
        batch(0, "low", 0), once(-2, "gn_var", 1), group(6, "logit_max"), group(6, "logit_exp"), group(5, "dev", 1),
        batch(1, "score", 1), once(4, "image", 3), group(7, "route"), once(-2, "gn_mean", 2), batch(-1, "pv"),
        once(-6, "xT", 3), group(4, "mean", 0), batch(2, "split_z"), batch(0, "low", 1), once(3, "gn_var", 3),
        batch(1, "score", 3), once(3, "image_low", 2), batch(0, "prob", 2), batch(1, "score", 4), once(-2, "normalise", 1),
        batch(4, "leak"), batch(0, "prob", 3), once(3, "normalise", 3), once(-4, "dnT", 0), batch(1, "minus_max"),
        batch(3, "down"), once(-2, "small", 1), batch(1, "zV"), once(-1, "image_low", 1), group(7, "wT"), group(5, "uT"),
        batch(0, "low", 2), batch(2, "zK"), batch(0, "low", 3), once(-3, "gn_mean", 1), once(-3, "small", 0),
        once(-2, "small", 2), once(13, "w1", 0), once(-2, "gn_var", 2), once(0, "gn_mean", 3), group(4, "dev", 0),
        once(1, "normalise", 2), batch(1, "shift"), batch(0, "prob", 4), once(-5, "xT", 1), batch(4, "y_split"),
        once(18, "w1", 2), batch(3, "tok"), group(2, "proj", 0), batch(2, "yQ"), group(4, "proj", 1),
        once(5, "image_low", 3), group(5, "logits"), once(14, "w1", 1), group(7, "pool"), once(2, "image", 2),
        batch(1, "prob", 0)]
LAST = [("hidden", 0), ("dev", G - 1, 1), ("uT", G - 1), ("experts", 0), ("logits", G - 1), ("logit_max", G - 1), ("logit_exp", G - 1),
        ("turned", 0), ("select", G - 1), ("route", G - 1), ("scatter", 1), ("wT", G - 1), ("pool", G - 1), ("scatter", 2), ("hidden", 1),
        ("scatter", 0), ("experts", 1), ("turned", 1), ("scatter", G - 1)]


def schedule():
    events = list(FIRST)
    for t in range(-6, B + 4):
        for event in STEP:
            e = event(t)
            if e is not None and e not in LAST:
                events.append(e)
    return events + LAST


EVENTS = schedule()
ON_A = ("xT", "small", "dnT", "gn_mean", "gn_var", "proj", "score", "uT", "shift", "down", "wT", "pool", "yQ",
        "experts", "turned", "scatter")
ON_B = ("up", "prob", "logits", "pv", "tok", "zK", "zV", "hidden")
A = {e: n for n, e in enumerate(e for e in EVENTS if e[0] in ON_A)}
BU = {e: n for n, e in enumerate(e for e in EVENTS if e[0] in ON_B)}
BANKS = 4
ONE_BANK = ("gn_mean", "gn_var", "dnT", "shift", "down", "wT", "pool", "experts", "turned", "tok", "zK", "zV", "hidden")


def place(units):
    bank, user, out = 0, [None] * BANKS, {}
    for n, e in enumerate(units):
        size = 1 if e[0] in ONE_BANK or (e[0] in ("score", "prob") and e[2] == NU - 1) else 2
        if bank + size > BANKS:
            bank = 0
        before = [user[b] for b in range(bank, bank + size) if user[b] is not None]
        out[e] = bank, size, max(before) if before else None
        user[bank:bank + size] = [n] * size
        bank = (bank + size) % BANKS
    return out


def nth(*event):
    return [e for e in EVENTS if e[0] == event[0]].index(event) + 1


PLACES = {**place(A), **place(BU)}
LOWS = [(n, i) for n in range(B) for i in range(NU)]


def pool_takes(n, i):
    return i in POOL_LOW and n < B - 1


def hybrid_kernel(nc, x, bias, up_filter, dn_filter, Wq, Wk, Wv, gate_w, gate_b, weight1, weight2, out):
    def by_token(v):
        return v.rearrange("b h w c -> b (h w) c").rearrange("(g b) (a p r) c -> g p b a (r c)", g=G, a=2, r=R)

    x_tokens, out_tokens = by_token(x), by_token(out)
    cst_dram = nc.inline_tensor(constants(), name="shape_constants").ap()
    tables = nc.dram_tensor("filter_tables", (2, AROWS, TROW), F32, kind="Internal").ap()

    with ExitStack() as ctx:
        def sb(name, shape, dt=F32):
            return ctx.enter_context(nc.sbuf_tensor(name, shape, dt))

        def sem(name):
            return ctx.enter_context(nc.semaphore(name))

        cst = sb("cst", [P, C_COLS])
        ident = cst[:, C_ID:C_ID + P]
        ident_b = sb("ident_b", [P, P], BF16)
        mask_b = sb("mask_b", [P, P], BF16)
        ident_h = sb("ident_h", [P, P], F16)
        x_all = sb("x_all", [P, G, SLOT])
        xF_all = sb("xF_all", [P, G, SLOT])
        xin = sb("xin", [P, 2, SLOT])
        biasr = sb("biasr", [P, H])
        stats = sb("stats", [P, 6])
        mv = sb("mv", [P, G, GB, 2])
        gmean = sb("gmean", [P, G, GB])
        gvar = sb("gvar", [P, G, GB])
        grstd = sb("grstd", [P, G, GB])
        gdiff = sb("gdiff", [P, GB])
        pads = sb("pads", [32, 2, TROW])
        dnrow = sb("dnrow", [32, TAPS])
        UU = sb("UU", [P, 2, SPAN, 2, 2 * W], F16)
        D = sb("D", [P, NS, C])
        D_parts = sb("D_parts", [P, 2, NS, C], F16)
        DD = sb("DD", [P, 2, SPAN, R, C], F16)
        y32 = sb("y32", [P, SLOT])
        y = sb("y", [P, 2, SLOT])
        positive = sb("positive", [P, SLOT])
        tF = sb("tF", [P, SLOT])
        sq_z = sb("sq_z", [P, BC])
        centred = sb("centred", [P, BC])
        zss = sb("zss", [P, KT])
        zrstd = sb("zrstd", [P, KT])
        z32 = sb("z32", [P, KT, C])
        z4 = sb("z4", [P, 2, KT, 4, C], F16)
        zK = sb("zK", [P, 3, S], F16)
        yQ = sb("yQ", [P, 3, S], F16)
        zV = sb("zV", [P, 3, KT, 2 * C], F16)
        negmax = sb("negmax", [P, 2, KT])
        M4 = sb("M4", [P, KT, 4, C], F16)
        e32 = sb("e32", [P, 3, SLOT])
        Pp = sb("Pp", [P, 2, 2, PCOLS], F16)
        oT = sb("oT", [P, 2, S])
        t2_all = sb("t2_all", [P, G, SLOT])
        uT = sb("uT", [P, S])
        att = uT
        rsum = sb("rsum", [P, 2, KT, 2])
        nmean = sb("nmean", [P, 2, 2 * KT])
        uss = sb("uss", [P, 2 * KT])
        urstd = sb("urstd", [P, 2 * KT])
        sq_u = sb("sq_u", [P, 2 * BC])
        u = sb("u", [P, KT, P])
        lg = sb("lg", [GE, S])
        probs = sb("probs", [GE, S])
        rest = sb("rest", [GE, S])
        top8 = sb("top8", [GE, TOP])
        ntop = sb("ntop", [GE, 1])
        esum = sb("esum", [GE, 1])
        inverse = sb("inverse", [GE, 1])
        wT = sb("wT", [P, KT, GE])
        pooled32 = sb("pooled32", [C, E_, GB])
        pooled = sb("pooled", [3 * C + 2, E_, B], F16)
        wq_sb = sb("wq_sb", [C, C])
        wk_sb = sb("wk_sb", [C, C])
        wv_sb = sb("wv_sb", [C, C])
        gw_sb = sb("gw_sb", [E_, GB, C])
        gb_sb = sb("gb_sb", [GE, 1])
        wvT = sb("wvT", [C, C])
        A_sb = sb("A_sb", [C, C])
        T1 = sb("T1", [C, R, C])
        gateT = sb("gateT", [P, GB, E_])
        V2 = sb("V2", [P, 2 * C + 2])
        Bs = sb("Bs", [P, C])
        BB = sb("BB", [P, 4, C], F16)
        w2bias = sb("w2bias", [C, E_])
        power = sb("power", [P, 1])
        hid = sb("hid", [HID, E_, B])
        o2 = sb("o2", [C, B, E_])
        obd = sb("obd", [GE, G, GB, C])
        early = Pp[:, :, :, :].rearrange("p i j n -> p (i j n)").bitcast(F32)

        def early_part(rows, at, n, a):
            return early[0:rows, at:at + a * n].rearrange("p (a t) -> p a t", a=a)

        upE = early_part(P, 0, EW, AROWS)
        upD = early_part(P, 1024, 2 * W, AROWS)
        dnE = early_part(C, 2048, 2 * W, AROWS)
        U = early[:, 3072:3072 + NS * P].rearrange("p (m q t) -> p m q t", m=NS, q=2)
        U_parts = early[:, 4096:4096 + NS * P].bitcast(F16).rearrange("p (i m q t) -> p i m q t", i=2, m=NS, q=2)
        img = [[xin[:, i, :].bitcast(F16)[:, SLOT * j:SLOT * j + SLOT] for j in range(2)] for i in range(2)]
        y_parts = [[y[:, i, :].bitcast(F16)[:, SLOT * j:SLOT * j + SLOT] for j in range(2)] for i in range(2)]
        yflat = y[:, :, :].rearrange("p i n -> p (i n)")
        w1_sb = yflat[0:3 * C + 2].rearrange("p (e h) -> p e h", e=E_)
        w1_parts = positive[:, :].bitcast(F16)[0:3 * C + 2].rearrange("p (e h) -> p e h", e=E_)
        w2_sb = xin[:, 0, 0:E_ * C].rearrange("p (e c) -> p e c", e=E_)

        psA = ctx.enter_context(nc.psum_tensor("psA", [P, BANKS * BANK], F32))
        psB = ctx.enter_context(nc.psum_tensor("psB", [P, BANKS * BANK], F32))

        def slot(e):
            bank, size, _ = PLACES[e]
            return (psA if e in A else psB)[:, BANK * bank:BANK * (bank + size)]

        x_loaded = [sem(f"x_loaded{g}") for g in range(G)]
        cst_loaded = sem("cst_loaded")
        proj_loaded = sem("proj_loaded")
        ffn_loaded = sem("ffn_loaded")
        w2bias_loaded = sem("w2bias_loaded")
        w1_high, w1_split = sem("w1_high"), sem("w1_split")
        filters_loaded = sem("filters_loaded")
        dn_reversed = sem("dn_reversed")
        tables_stored = sem("tables_stored")
        toeplitz_loaded = sem("toeplitz_loaded")
        dn_toeplitz_loaded = sem("dn_toeplitz_loaded")
        pads_zero = sem("pads_zero")
        fills_ready = sem("fills_ready")
        power_ready = sem("power_ready")
        masks_ready = sem("masks_ready")
        a_filled, a_drained = sem("a_filled"), sem("a_drained")
        b_filled, b_drained = sem("b_filled"), sem("b_drained")
        U_ready = sem("U_ready")
        UU_ready = sem("UU_ready")
        stats_ready = sem("stats_ready")
        g_rstd = sem("g_rstd")
        xn_ready = sem("xn_ready")
        xin_sum, xin_high, xin_ready = sem("xin_sum"), sem("xin_high"), sem("xin_ready")
        U_split = sem("U_split")
        y_leaked, y_rounded, y_ready = sem("y_leaked"), sem("y_rounded"), sem("y_ready")
        z_squared = sem("z_squared")
        z_var, z_rstd = sem("z_var"), sem("z_rstd")
        z_scaled, z_split = sem("z_scaled"), sem("z_split")
        z4_ready = sem("z4_ready")
        q_high = sem("q_high")
        max_ready = sem("max_ready")
        low_by_dve, low_by_pool = sem("low_by_dve"), sem("low_by_pool")
        t2_mean = sem("t2_mean")
        t2_centred = sem("t2_centred")
        t2_squared = sem("t2_squared")
        t2_var = sem("t2_var")
        t2_rstd = sem("t2_rstd")
        u_ready = sem("u_ready")
        lg_max = sem("lg_max")
        lg_exp = sem("lg_exp")
        route_ready = sem("route_ready")
        inverse_ready, p_scaled = sem("inverse_ready"), sem("p_scaled")
        pooled_split = sem("pooled_split")
        half_filled, half_ready = sem("half_filled"), sem("half_ready")
        stored = sem("stored")
        dve_chain = sem("dve_chain")

        def by_pairs(v, i):
            return v[:, 2 * BC * i:2 * BC * (i + 1)].rearrange("p (b k c) -> p b k c", b=2, k=KT)

        def per_token(v):
            return v.rearrange("p (b k) -> p b k", b=2).unsqueeze(3).broadcast_to([P, 2, KT, C])

        def pair_of_u(i):
            return u[:, :, 2 * C * i:2 * C * (i + 1)].rearrange("p k (b c) -> p b k c", b=2)

        def low_part(queue, engine, n, i):
            N, o = UCOLS[i], UOFF[i]
            queue.wait_ge(b_drained, BU["prob", n, i] + 1)
            return engine.tensor_tensor(Pp[:, n % 2, 1, o:o + N], e32[:, (NU * n + i) % 3, 0:N], Pp[:, n % 2, 0, o:o + N], ALU.subtract)

        def low_count(n, i):
            mine = [m for m in LOWS[:NU * n + i + 1] if pool_takes(*m) == pool_takes(n, i)]
            return (low_by_pool if pool_takes(n, i) else low_by_dve), len(mine)

        block = ctx.enter_context(nc.Block())

        @block.sync
        def _(sp):
            sp.dma_start(x_all[:, 0, :].rearrange("p (b a n) -> p b a n", b=GB, a=2), x_tokens[0]).then_inc(x_loaded[0], 16)
            sp.dma_start(cst[:, :], cst_dram).then_inc(cst_loaded, 16)
            sp.dma_start(wq_sb[:, :], Wq).then_inc(proj_loaded, 16)
            sp.dma_start(wk_sb[:, :], Wk).then_inc(proj_loaded, 16)
            sp.dma_start(wv_sb[:, :], Wv).then_inc(proj_loaded, 16)
            for b in range(GB):
                sp.dma_start(gw_sb[:, b, :], gate_w).then_inc(proj_loaded, 16)
            sp.wait_ge(toeplitz_loaded, 16 * R)
            for g in range(1, G):
                sp.dma_start(x_all[:, g, :].rearrange("p (b a n) -> p b a n", b=GB, a=2), x_tokens[g]).then_inc(x_loaded[g], 16)
            with nc.allow_non_contiguous_dma(reason="a small transposed bias"):
                sp.dma_start(w2bias[:, :], weight2[:, HID, :].rearrange("e o -> o e")).then_inc(w2bias_loaded, 16)
            for b in range(GB):
                sp.dma_start(gb_sb[E_ * b:E_ * b + E_, :], gate_b.rearrange("(e a) -> e a", a=1)).then_inc(proj_loaded, 16)
            sp.wait_ge(a_filled, A["down", B - 1] + 1)
            for i in range(3):
                sp.dma_start(w1_sb[C * i:C * i + C], weight1[:, 0:C, :].rearrange("e d h -> d e h")).then_inc(ffn_loaded, 16)
            for i in range(2):
                sp.dma_start(w1_sb[3 * C + i:3 * C + i + 1], weight1[:, C:C + 1, :].rearrange("e d h -> d e h")).then_inc(ffn_loaded, 16)
            sp.dma_start(w2_sb, weight2[:, 0:HID, :].rearrange("e h o -> h e o")).then_inc(ffn_loaded, 16)
            for g in [e[1] for e in EVENTS if e[0] == "scatter"]:
                for a in range(2):
                    if a == 0:
                        sp.wait_ge(half_ready, nth("scatter", g))
                    else:
                        sp.wait_ge(a_drained, A["scatter", g] + 1)
                    sp.dma_start(out_tokens[g][:, :, a], x_all[:, g, :].rearrange("p (b a n) -> p b a n", b=GB, a=2)[:, :, a]).then_inc(stored, 16)
            sp.wait_ge(stored, 16 * 2 * G)

        @block.gpsimd
        def _(pool):
            nc.gpsimd.memset(pads[:, :, :], 0.0).then_inc(pads_zero, 1)
            nc.gpsimd.memset(dnrow[:, :], 0.0).then_inc(pads_zero, 1)
            nc.gpsimd.memset(power[:, :], -0.5).then_inc(power_ready, 1)
            nc.gpsimd.memset(UU[:, :, :, :, :], 0.0).then_inc(fills_ready, 1)
            nc.gpsimd.memset(DD[:, :, :, :, :], 0.0).then_inc(fills_ready, 1)
            nc.gpsimd.memset(z32[:, :, :], 1.0).then_inc(fills_ready, 1)
            nc.gpsimd.memset(M4[:, :, :, :], 0.0).then_inc(fills_ready, 1)
            nc.gpsimd.memset(pooled[:, :, :], 1.0).then_inc(fills_ready, 1)
            pool.wait_ge(power_ready, 1)

            def inverse_root(v, n):
                return nc.gpsimd.tensor_tensor(v, v, power[:, 0:1].broadcast_to([P, n]), ALU.pow)

            def image_input(g):
                for i, (lo, hi) in enumerate(PIECES):
                    pool.wait_ge(xn_ready, 2 * nth("normalise", g) - 1 + i)
                    if g == 0 and i == 0:
                        pool.wait_ge(filters_loaded, 48)
                    v = x_all[:, g, lo:hi].rearrange("p (b h j) -> p b h j", h=H, j=JW)
                    shared = biasr[:, :].unsqueeze(1).unsqueeze(3).broadcast_to([P, (hi - lo) // BC, H, JW])
                    nc.gpsimd.tensor_tensor(v, v, shared, ALU.add).then_inc(xin_sum, 1)

            for e in EVENTS:
                name, g = e[0], e[1]
                if name == "gn_var":
                    pool.wait_ge(a_drained, A["gn_var", g] + 1)
                    inverse_root(grstd[:, g, :], GB).then_inc(g_rstd, 1)
                elif name == "image":
                    image_input(g)
                elif name == "leak":
                    pool.wait_ge(b_drained, BU["up", g] + 1)
                    nc.gpsimd.tensor_tensor(y32[:, :], y32[:, :], positive[:, :], ALU.add).then_inc(y_leaked, 1)
                elif name == "low" and pool_takes(*e[1:]):
                    low_part(pool, nc.gpsimd, g, e[2]).then_inc(low_by_pool, 1)
                elif name == "z_rstd":
                    pool.wait_ge(z_var, g + 1)
                    inverse_root(zrstd[:, :], KT).then_inc(z_rstd, 1)
                elif name == "split_z":
                    pool.wait_ge(z_split, g + 1)
                    nc.gpsimd.tensor_copy(z4[:, g % 2, :, 2:4, :], z4[:, g % 2, :, 0:2, :]).then_inc(z4_ready, 1)
                elif name == "mean" and e[1:] != LAST_PAIR:
                    pool.wait_ge(t2_mean, 2 * g + e[2] + 1)
                    if g >= 1:
                        pool.wait_ge(a_filled, A["pool", g - 1] + 1)
                    nc.gpsimd.tensor_tensor(pair_of_u(e[2]), by_pairs(t2_all[:, g, :], e[2]), per_token(nmean[:, e[2], :]), ALU.add).then_inc(t2_centred, 1)
                elif name == "dev":
                    pool.wait_ge(t2_var, 2 * g + e[2] + 1)
                    inverse_root(urstd[:, :], 2 * KT).then_inc(t2_rstd, 1)
                    if e[1:] != LAST_PAIR:
                        pool.wait_ge(t2_rstd, 2 * g + e[2] + 1)
                        nc.gpsimd.tensor_tensor(pair_of_u(e[2]), pair_of_u(e[2]), per_token(urstd[:, :]), ALU.mult).then_inc(u_ready, 1)

        @block.scalar
        def _(act):
            act.wait_ge(pads_zero, 2)
            act.dma_start(pads[2:2 + TAPS, 0, UP_AT:UP_AT + TAPS], up_filter[0, 0]).then_inc(filters_loaded, 16)
            act.dma_start(dnrow[2:2 + TAPS, :], dn_filter[0, 0]).then_inc(filters_loaded, 16)
            act.dma_start(biasr[:, :], bias.rearrange("a h c d -> a (h c d)").broadcast_to([P, H])).then_inc(filters_loaded, 16)
            act.wait_ge(filters_loaded, 48)
            act.wait_ge(dn_reversed, 1)
            act.dma_start(tables.rearrange("f a t -> a f t"), pads[0:AROWS, :, :]).then_inc(tables_stored, 16)
            act.wait_ge(tables_stored, 16)
            up_src = bass.AP(tensor=tables.tensor, offset=0, ap=[[2, C], [TROW, AROWS], [1, EW]])
            dn_src = bass.AP(tensor=tables.tensor, offset=AROWS * TROW, ap=[[2, C], [TROW, AROWS], [1, 2 * W]])
            for b in range(R):
                act.dma_start(upE[C * b:C * b + C, :, :], up_src).then_inc(toeplitz_loaded, 16)
            act.dma_start(dnE[:, :, :], dn_src).then_inc(dn_toeplitz_loaded, 16)

            for e in EVENTS:
                name, n = e[0], e[1]
                if e in BU:
                    act.wait_ge(b_filled, BU[e] + 1)
                if name == "image":
                    if n >= 2:
                        act.wait_ge(b_filled, BU["up", GB * (n - 1) - 1] + 1)
                    for i, (lo, hi) in enumerate(PIECES):
                        act.wait_ge(xin_sum, 2 * n + 1 + i)
                        nc.scalar.activation(img[n % 2][0][:, lo:hi], x_all[:, n, lo:hi], ACT.Copy).then_inc(xin_high, 1)
                if name == "up":
                    if n >= 1:
                        act.wait_ge(y_ready, n)
                    nc.scalar.activation(y32[:, :], slot(e), ACT.Copy, scale=SLOPE / UP_SCALE)
                    nc.scalar.activation(positive[:, :], slot(e), ACT.Relu, scale=(1.0 - SLOPE) / UP_SCALE).then_inc(b_drained, 1)
                elif name == "tok":
                    g, b = n // GB, n % GB
                    nc.scalar.activation(t2_all[:, g, BC * b:BC * b + BC], slot(e)[:, 0:BC], ACT.Copy)
                    if n >= 1:
                        act.wait_ge(z_var, n)
                    nc.scalar.activation(sq_z[:, :], slot(e)[:, BC:2 * BC], ACT.Square).then_inc(z_squared, 1)
                    if n >= 1:
                        act.wait_ge(z_split, n)
                    nc.scalar.activation(centred[:, :], slot(e)[:, BC:2 * BC], ACT.Copy).then_inc(b_drained, 1)
                elif name == "zK":
                    src = slot(e).bitcast(F16)[:, 0:S].rearrange("p (a r q) -> p a r q", a=2, r=R)
                    nc.scalar.activation(zK[:, n % 3, :].rearrange("p (a q r) -> p a r q", a=2, r=R), src,
                                         ACT.Copy).then_inc(b_drained, 1)
                elif name == "zV":
                    nc.scalar.activation(zV[:, n % 3, :, :].rearrange("p k d -> p (k d)"), slot(e).bitcast(F16)[:, 0:KT * 2 * C],
                                         ACT.Copy).then_inc(b_drained, 1)
                elif name == "yQ":
                    act.wait_ge(a_filled, A[e] + 1)
                    nc.scalar.activation(yQ[:, n % 3, :], slot(e), ACT.Copy).then_inc(q_high, 1)
                elif name == "prob":
                    m = NU * n + e[2]
                    if m >= 3:
                        act.wait_ge(*low_count((m - 3) // NU, (m - 3) % NU))
                    N = UCOLS[e[2]]
                    nc.scalar.activation(e32[:, m % 3, 0:N], slot(e)[:, 0:N], ACT.Exp)
                    nc.scalar.activation(Pp[:, n % 2, 0, UOFF[e[2]]:UOFF[e[2]] + N], slot(e)[:, 0:N], ACT.Exp).then_inc(b_drained, 1)
                elif name == "pv":
                    nc.scalar.activation(oT[64 * (n % 2):64 * (n % 2) + 64, n // 2 % 2, :], slot(e)[0:64, :],
                                         ACT.Copy).then_inc(b_drained, 1)
                elif name == "mean":
                    m = 2 * n + e[2]
                    act.wait_ge(t2_centred, m + 1)
                    if m >= 1:
                        act.wait_ge(t2_var, m)
                    nc.scalar.activation(sq_u[:, :].rearrange("p (b k c) -> p b k c", b=2, k=KT), pair_of_u(e[2]), ACT.Square).then_inc(t2_squared, 1)
                elif name == "logits":
                    nc.scalar.activation(lg[:, :], slot(e)[0:GE, :], ACT.Identity, bias=gb_sb[:, 0:1]).then_inc(b_drained, 1)
                elif name == "logit_exp":
                    act.wait_ge(lg_max, n + 1)
                    nc.scalar.activation(probs[:, :], lg[:, :], ACT.Exp, bias=ntop[:, 0:1],
                                         accum_out=esum[:, 0:1]).then_inc(lg_exp, 1)
                elif name == "route":
                    act.wait_ge(inverse_ready, n + 1)
                    nc.scalar.activation(probs[:, :], probs[:, :], ACT.Copy, scale=inverse[:, 0:1]).then_inc(p_scaled, 1)
                elif name == "hidden":
                    first, last = PARTS[n]
                    nc.scalar.activation(hid[:, :, first:last], slot(e)[:, 0:E_ * B].rearrange("p (e b) -> p e b", e=E_)[:, :, first:last],
                                         ACT.Gelu).then_inc(b_drained, 1)

        @block.vector
        def _(dve):
            chained = [0]

            def link(ins):
                chained[0] += 1
                ins.then_inc(dve_chain, 1)
                dve.wait_ge(dve_chain, chained[0])

            def blocks(n, m, like, first=C_BD):
                return cst[0:like, first:first + n].unsqueeze(2).broadcast_to([like, n, m])

            dve.wait_ge(filters_loaded, 48)
            nc.vector.tensor_copy(pads[:, 1, DN_AT:DN_AT + TAPS], dnrow[:, ::-1]).then_inc(dn_reversed, 1)
            dve.wait_ge(cst_loaded, 16)
            nc.vector.tensor_copy(ident_b[:, :], ident).then_inc(masks_ready, 1)
            nc.vector.tensor_copy(mask_b[:, :], cst[:, C_MASK:C_MASK + P]).then_inc(masks_ready, 1)
            nc.vector.tensor_copy(ident_h[:, :], ident).then_inc(masks_ready, 1)

            for e in EVENTS:
                name, n = e[0], e[1]
                if e in A and name not in ("yQ", "scatter"):
                    dve.wait_ge(a_filled, A[e] + 1)
                s = slot(e) if e in A else None
                if name == "xT":
                    nc.vector.tensor_copy(xF_all[:, n, :], s).then_inc(a_drained, 1)
                    dve.wait_ge(a_drained, A[e] + 1)
                    for b in range(GB):
                        link(nc.vector.bn_stats(stats[:, :], xF_all[:, n, BC * b:BC * b + BC]))
                        ins = nc.vector.bn_aggr(mv[:, n, b, :], stats[:, :])
                        if b < GB - 1:
                            link(ins)
                    ins.then_inc(stats_ready, 1)
                elif name == "gn_mean":
                    link(nc.vector.tensor_copy(gmean[:, n, :], s[:, 0:GB]))
                    link(nc.vector.tensor_tensor(gdiff[:, :], mv[:, n, :, 0], gmean[:, n, :], ALU.subtract))
                    link(nc.vector.tensor_tensor(gdiff[:, :], gdiff[:, :], gdiff[:, :], ALU.mult))
                    nc.vector.tensor_tensor(gvar[:, n, :], mv[:, n, :, 1], gdiff[:, :], ALU.add).then_inc(a_drained, 1)
                elif name == "gn_var":
                    nc.vector.tensor_scalar(grstd[:, n, :], s[:, 0:GB], EPS, None, ALU.add).then_inc(a_drained, 1)
                elif name == "normalise":
                    dve.wait_ge(g_rstd, nth("gn_var", n))
                    for b in range(GB):
                        r = slice(BC * b, BC * b + BC)
                        ins = nc.vector.tensor_scalar(x_all[:, n, r], xF_all[:, n, r], gmean[:, n, b:b + 1], grstd[:, n, b:b + 1],
                                                      ALU.subtract, ALU.mult)
                        if b in (0, GB - 1):
                            ins.then_inc(xn_ready, 1)
                elif name == "U":
                    dve.wait_ge(toeplitz_loaded, 16 * R)
                    link(nc.vector.tensor_tensor(upD, upE[:, :, 0:2 * W], upE[:, :, 1:2 * W + 1], ALU.add))
                    nc.vector.tensor_tensor(U[:, :, 0, :], upD[:, 1:2 * NS:2, :], upD[:, 2:2 * NS + 1:2, :], ALU.add).then_inc(U_ready, 1)
                    nc.vector.tensor_tensor(U[:, :, 1, :], upD[:, 0:2 * NS - 1:2, :], upD[:, 1:2 * NS:2, :], ALU.add).then_inc(U_ready, 1)
                    dve.wait_ge(U_ready, 2)
                    high, low = U_parts[:, 0, :, :, :], U_parts[:, 1, :, :, :]
                    nc.vector.tensor_scalar(high, U, UP_SCALE, None, ALU.mult).then_inc(U_split, 1)
                    dve.wait_ge(U_split, 1)
                    nc.vector.scalar_tensor_tensor(out=low, in0=U, scalar=UP_SCALE, in1=high, op0=ALU.mult, op1=ALU.subtract).then_inc(U_split, 1)
                elif name == "UU":
                    dve.wait_ge(fills_ready, 5)
                    dve.wait_ge(U_split, 2)
                    for r in range(R):
                        q = slice(C * r, C * r + C)
                        nc.vector.tensor_copy(UU[q, :, R - 1 - r:R - 1 - r + NS, :, :].rearrange("p i m q t -> p i (m q t)"),
                                              U_parts[q, :, :, :, :].rearrange("p i m q t -> p i (m q t)")).then_inc(UU_ready, 1)
                elif name == "image_low":
                    for i, (lo, hi) in enumerate(PIECES):
                        dve.wait_ge(xin_high, 2 * n + 1 + i)
                        nc.vector.tensor_tensor(img[n % 2][1][:, lo:hi], x_all[:, n, lo:hi], img[n % 2][0][:, lo:hi],
                                                ALU.subtract).then_inc(xin_ready, 1)
                elif name == "small" and n == 0:
                    link(nc.vector.tensor_copy(wvT[:, :], s[0:C, 0:C]))
                    link(nc.vector.tensor_copy(A_sb[:, :], s[0:C, P:P + C]))
                    nc.vector.tensor_tensor(gateT[:, :, :], s[:, BANK:BANK + E_].unsqueeze(1).broadcast_to([P, GB, E_]),
                                            blocks(GB, E_, P), ALU.mult).then_inc(a_drained, 1)
                elif name == "small" and n == 1:
                    link(nc.vector.tensor_copy(T1[:, :, :], s[0:C, 0:C].unsqueeze(1).broadcast_to([C, R, C])))
                    link(nc.vector.tensor_copy(V2[:, 2 * C:2 * C + 2], cst[:, C_SUM:C_SUM + 2]))
                    nc.vector.tensor_tensor(V2[:, 0:2 * C].rearrange("p (b c) -> p b c", b=2), s[:, BANK:BANK + C].unsqueeze(1).broadcast_to([P, 2, C]),
                                            blocks(2, C, P, C_HALF), ALU.mult).then_inc(a_drained, 1)
                elif name == "small":
                    link(nc.vector.tensor_scalar(Bs[:, :], s[:, 0:C], float(C) ** -0.5, None, ALU.mult))
                    link(nc.vector.tensor_copy(BB[:, :, :], Bs[:, :].unsqueeze(1).broadcast_to([P, 4, C])))
                    nc.vector.tensor_tensor(BB[2 * C:P, :, :], Bs[2 * C:P, :].unsqueeze(1).broadcast_to([2 * C, 4, C]),
                                            BB[2 * C:P, :, :], ALU.subtract).then_inc(a_drained, 1)
                elif name == "dnT":
                    link(nc.vector.tensor_copy(D[:, :, :], s[:, 0:NS * C].rearrange("p (m c) -> p m c", m=NS)))
                    link(nc.vector.tensor_scalar(D_parts[:, 0, :, :], D[:, :, :], DOWN_SCALE, None, ALU.mult))
                    link(nc.vector.scalar_tensor_tensor(out=D_parts[:, 1, :, :], in0=D[:, :, :], scalar=DOWN_SCALE, in1=D_parts[:, 0, :, :],
                                                        op0=ALU.mult, op1=ALU.subtract))
                    for r in range(R):
                        ins = nc.vector.tensor_copy(DD[:, :, r:r + NS, r, :], D_parts[:, :, :, :])
                    ins.then_inc(a_drained, 1)
                elif name == "y_split":
                    high, low = y_parts[n % 2]
                    dve.wait_ge(y_leaked, n + 1)
                    if n >= 2:
                        dve.wait_ge(a_filled, A["down", n - 2] + 1)
                    nc.vector.tensor_copy(high, y32[:, :]).then_inc(y_rounded, 1)
                    dve.wait_ge(y_rounded, n + 1)
                    nc.vector.tensor_tensor(low, y32[:, :], high, ALU.subtract).then_inc(y_ready, 1)
                elif name == "down":
                    b = n % GB
                    nc.vector.scalar_tensor_tensor(out=tF[:, BC * b:BC * b + BC], in0=s[:, 0:BC], scalar=GAIN / DOWN_SCALE,
                                                   in1=xF_all[:, n // GB, BC * b:BC * b + BC], op0=ALU.mult, op1=ALU.add).then_inc(a_drained, 1)
                elif name == "z_rstd":
                    dve.wait_ge(z_squared, n + 1)
                    link(nc.vector.tensor_reduce(zss[:, :], sq_z[:, :].rearrange("p (n c) -> p n c", c=C), X, ALU.add))
                    nc.vector.tensor_scalar(zrstd[:, :], zss[:, :], 1.0 / C, EPS, ALU.mult, ALU.add).then_inc(z_var, 1)
                elif name == "split_z":
                    s = centred[:, :].rearrange("p (n c) -> p n c", c=C)
                    dve.wait_ge(b_drained, BU["tok", n] + 1)
                    dve.wait_ge(z_rstd, n + 1)
                    if n >= 2:
                        dve.wait_ge(b_filled, BU["zK", n - 2] + 1)
                    nc.vector.tensor_tensor(z32[:, :, 0:C - 1], s[:, :, 0:C - 1],
                                            zrstd[:, :].unsqueeze(2).broadcast_to([P, KT, C - 1]), ALU.mult).then_inc(z_scaled, 1)
                    dve.wait_ge(z_scaled, n + 1)
                    link(nc.vector.tensor_copy(z4[:, n % 2, :, 0, :], z32[:, :, :]))
                    nc.vector.tensor_tensor(z4[:, n % 2, :, 1, :], z32[:, :, :], z4[:, n % 2, :, 0, :], ALU.subtract).then_inc(z_split, 1)
                elif name == "yQ":
                    dve.wait_ge(q_high, n + 1)
                    v = yQ[2 * C:P, n % 3, :]
                    nc.vector.tensor_tensor(v, s[2 * C:P, :], v, ALU.subtract).then_inc(a_drained, 1)
                elif name == "score":
                    for k, (m, at) in enumerate(packed(e[2])):
                        ins = nc.vector.tensor_reduce(negmax[:, n % 2, m - 1:m], s[:, at:at + P * m], X, ALU.max, negate=True)
                    ins.then_inc(a_drained, 1)
                elif name == "minus_max":
                    dve.wait_ge(a_drained, max(A["score", n, i] for i in range(NU)) + 1)
                    v = negmax[:, n % 2, :].unsqueeze(2).broadcast_to([P, KT, 2])
                    link(nc.vector.tensor_copy(M4[:, :, 0:2, C - 1], v))
                    nc.vector.tensor_tensor(M4[:, :, 2:4, C - 1], v, M4[:, :, 0:2, C - 1], ALU.subtract).then_inc(max_ready, 1)
                elif name == "shift":
                    v = yQ[:, n % 3, :]
                    nc.vector.tensor_tensor(v, v, s.bitcast(F16)[:, 0:S], ALU.add).then_inc(a_drained, 1)
                elif name == "low" and not pool_takes(*e[1:]):
                    low_part(dve, nc.vector, n, e[2]).then_inc(low_by_dve, 1)
                elif name == "proj":
                    sv = s.rearrange("p (k d) -> p k d", k=KT)
                    av = att[:, :].rearrange("p (b k c) -> p k b c", b=GB, k=KT)[:, :, 2 * e[2]:2 * e[2] + 2, :]
                    link(nc.vector.reciprocal(rsum[:, e[2], :, :], sv[:, :, 2 * C:2 * C + 2]))
                    nc.vector.tensor_tensor(av, sv[:, :, 0:2 * C].rearrange("p k (b c) -> p k b c", b=2),
                                            rsum[:, e[2], :, :].unsqueeze(3).broadcast_to([P, KT, 2, C]), ALU.mult).then_inc(a_drained, 1)
                elif name == "mean":
                    dve.wait_ge(a_drained, A["proj", n, e[2]] + 1)
                    dve.wait_ge(b_drained, BU["tok", GB * n + 2 * e[2] + 1] + 1)
                    v = t2_all[:, n, 2 * BC * e[2]:2 * BC * (e[2] + 1)]
                    link(nc.vector.tensor_tensor(v, v, att[:, 2 * BC * e[2]:2 * BC * (e[2] + 1)], ALU.add))
                    link(nc.vector.tensor_reduce(nmean[:, e[2], :], v.rearrange("p (n c) -> p n c", c=C), X, ALU.add))
                    nc.vector.tensor_scalar(nmean[:, e[2], :], nmean[:, e[2], :], -1.0 / C, None, ALU.mult).then_inc(t2_mean, 1)
                    if e[1:] == LAST_PAIR:
                        dve.wait_ge(t2_mean, 2 * G)
                        dve.wait_ge(a_filled, A["pool", n - 1] + 1)
                        nc.vector.tensor_tensor(pair_of_u(e[2]), by_pairs(t2_all[:, n, :], e[2]), per_token(nmean[:, e[2], :]),
                                                ALU.add).then_inc(t2_centred, 1)
                elif name == "dev":
                    m = 2 * n + e[2]
                    dve.wait_ge(t2_squared, m + 1)
                    if m >= 1:
                        dve.wait_ge(u_ready, m)
                    link(nc.vector.tensor_reduce(uss[:, :], sq_u[:, :].rearrange("p (n c) -> p n c", c=C), X, ALU.add))
                    nc.vector.tensor_scalar(urstd[:, :], uss[:, :], 1.0 / C, EPS, ALU.mult, ALU.add).then_inc(t2_var, 1)
                    if e[1:] == LAST_PAIR:
                        dve.wait_ge(t2_rstd, 2 * G)
                        nc.vector.tensor_tensor(pair_of_u(e[2]), pair_of_u(e[2]), per_token(urstd[:, :]), ALU.mult).then_inc(u_ready, 1)
                elif name == "uT":
                    nc.vector.tensor_copy(uT[:, :].rearrange("p (a q r) -> p a r q", a=2, r=R),
                                          s.rearrange("p (a r q) -> p a r q", a=2, r=R)).then_inc(a_drained, 1)
                elif name == "logit_max":
                    dve.wait_ge(b_drained, BU["logits", n] + 1)
                    link(nc.vector.max(top8[:, :], lg[:, :]))
                    nc.vector.tensor_scalar(ntop[:, :], top8[:, 0:1], -1.0, None, ALU.mult).then_inc(lg_max, 1)
                elif name == "select":
                    link(nc.vector.match_replace(rest[:, :], top8[:, :], lg[:, :], NEG))
                    dve.wait_ge(lg_exp, n + 1)
                    nc.vector.reciprocal(inverse[:, :], esum[:, :]).then_inc(inverse_ready, 1)
                elif name == "route":
                    dve.wait_ge(p_scaled, n + 1)
                    nc.vector.scalar_tensor_tensor(out=xF_all[0:GE, n, :], in0=rest[:, :], scalar=NEG, in1=probs[:, :],
                                                   op0=ALU.is_equal, op1=ALU.mult).then_inc(route_ready, 1)
                elif name == "w1":
                    if n == 0:
                        dve.wait_ge(ffn_loaded, 16 * 6)
                        nc.vector.tensor_copy(w1_parts, w1_sb).then_inc(w1_high, 1)
                    elif n == 1:
                        dve.wait_ge(w1_high, 1)
                        v = w1_parts[2 * C:3 * C]
                        nc.vector.tensor_tensor(v, w1_sb[2 * C:3 * C], v, ALU.subtract).then_inc(w1_split, 1)
                    else:
                        v = w1_parts[3 * C:3 * C + 2]
                        nc.vector.scalar_tensor_tensor(out=v, in0=v, scalar=cst[3 * C:3 * C + 2, C_ROW:C_ROW + 1], in1=w1_sb[3 * C:3 * C + 2],
                                                       op0=ALU.mult, op1=ALU.add).then_inc(w1_split, 1)
                elif name == "wT":
                    nc.vector.tensor_copy(wT[:, :, :].rearrange("p k n -> p (k n)"), s[:, 0:KT * GE]).then_inc(a_drained, 1)
                elif name == "pool":
                    for b in range(GB):
                        ins = nc.vector.tensor_copy(pooled32[:, :, b], s[C * b:C * b + C, E_ * b:E_ * b + E_])
                    ins.then_inc(a_drained, 1)
                    dve.wait_ge(a_drained, A["pool", n] + 1)
                    v = pooled[:, :, GB * n:GB * n + GB]
                    link(nc.vector.tensor_copy(v[0:C], pooled32[:, :, :]))
                    nc.vector.tensor_copy(v[2 * C:3 * C], pooled32[:, :, :]).then_inc(pooled_split, 1)
                    nc.vector.tensor_tensor(v[C:2 * C], pooled32[:, :, :], v[0:C], ALU.subtract).then_inc(pooled_split, 1)
                elif name == "experts":
                    first, last = PARTS[n]
                    if n == 0:
                        dve.wait_ge(w2bias_loaded, 16)
                    nc.vector.tensor_tensor(o2[:, first:last, :], s[0:C, E_ * first:E_ * last].rearrange("p (b e) -> p b e", e=E_),
                                            w2bias[:, :].unsqueeze(1).broadcast_to([C, last - first, E_]), ALU.add).then_inc(a_drained, 1)
                elif name == "turned":
                    groups = range(PARTS[n][0] // GB, PARTS[n][1] // GB)
                    for g in groups:
                        ins = nc.vector.tensor_tensor(obd[:, g, :, :], s[0:GE, C * g:C * g + C].unsqueeze(1).broadcast_to([GE, GB, C]),
                                                      blocks(GB, C, GE, C_BDE), ALU.mult)
                    ins.then_inc(a_drained, 1)
                elif name == "scatter":
                    for a in range(2):
                        tiles = slice(R * a, R * (a + 1))
                        if a == 0:
                            dve.wait_ge(half_filled, nth("scatter", n))
                        else:
                            dve.wait_ge(a_filled, A[e] + 1)
                        ins = nc.vector.tensor_tensor(x_all[:, n, :].rearrange("p (b k c) -> p k b c", b=GB, k=KT)[:, tiles],
                                                      s.rearrange("p (k b c) -> p k b c", b=GB, k=KT)[:, tiles],
                                                      t2_all[:, n, :].rearrange("p (b k c) -> p k b c", b=GB, k=KT)[:, tiles], ALU.add)
                        ins.then_inc(a_drained if a else half_ready, 1)

        @block.tensor
        def _(pe):
            def by_tile(v):
                w = v.rearrange("p (a q r) -> p a r q", a=2, r=R)
                return lambda k: w[:, k // R, k % R, :]

            def turn(s, src, idn, n=P):
                for k in range(KT):
                    ins = nc.tensor.transpose(s[:, n * k:n * k + n], src(k), idn)
                return ins

            def within(v, shift):
                return v.rearrange("p (h j) -> p h j", j=JW)[:, :, max(0, shift):JW + min(0, shift)]

            def convolve(out_cols, matrices):
                for i, (m, v, shift) in enumerate(sorted(matrices, key=lambda a: a[2] != 0)):
                    ins = nc.tensor.matmul(within(out_cols, -shift), m, within(v, shift), start=i == 0, stop=i == len(matrices) - 1)
                return ins

            def image_cols(n, k):
                at = BC * (n % GB) + P * k
                return tF[:, at:at + P]

            def pieces(first, last):
                cuts = [first] + [c for c in (BANK,) if first < c < last] + [last]
                return list(zip(cuts, cuts[1:]))

            pe.wait_ge(cst_loaded, 16)
            for e in EVENTS:
                name, n = e[0], e[1]
                if (e in A or e in BU) and PLACES[e][2] is not None:
                    pe.wait_ge(a_drained if e in A else b_drained, PLACES[e][2] + 1)
                s = slot(e) if e in A or e in BU else None
                if name == "xT":
                    pe.wait_ge(x_loaded[n], 16)
                    ins = turn(s, lambda k: x_all[:, n, P * k:P * k + P], ident)
                elif name == "gn_mean":
                    pe.wait_ge(stats_ready, nth("xT", n))
                    ins = nc.tensor.matmul(s[:, 0:GB], cst[:, C_AVG:C_AVG + P], mv[:, n, :, 0], start=True, stop=True)
                elif name == "gn_var":
                    pe.wait_ge(a_drained, A["gn_mean", n] + 1)
                    ins = nc.tensor.matmul(s[:, 0:GB], cst[:, C_AVG:C_AVG + P], gvar[:, n, :], start=True, stop=True)
                elif name == "small" and n == 0:
                    pe.wait_ge(proj_loaded, 16 * 11)
                    nc.tensor.matmul(s[0:C, 0:C], wv_sb[:, :], ident[0:C, 0:C], start=True, stop=True)
                    nc.tensor.matmul(s[0:C, P:P + C], wq_sb[:, :], wk_sb[:, :], start=True, stop=True)
                    ins = nc.tensor.matmul(s[:, BANK:BANK + E_], gw_sb[:, :, :], ident[0:E_, 0:E_], start=True, stop=True)
                elif name == "small" and n == 1:
                    pe.wait_ge(a_drained, A["small", 0] + 1)
                    nc.tensor.matmul(s[0:C, 0:C], A_sb[:, :], cst[0:C, C_Q:C_Q + C], start=True, stop=True)
                    ins = nc.tensor.matmul(s[:, BANK:BANK + C], cst[0:C, C_QREP:C_QREP + P], wvT[:, :], start=True, stop=True)
                elif name == "small":
                    pe.wait_ge(a_drained, A["small", 1] + 1)
                    ins = nc.tensor.matmul(s[:, 0:C], T1[:, :, :], cst[0:C, C_Q:C_Q + C], start=True, stop=True)
                elif name == "dnT":
                    pe.wait_ge(dn_toeplitz_loaded, 16)
                    rows = dnE.rearrange("p a t -> p (a t)")
                    for m in range(NS):
                        ins = nc.tensor.matmul(s[:, C * m:C * m + C], rows[:, 2 * W * (2 * m + 1):2 * W * (2 * m + 3)], ident[0:C, 0:C],
                                               start=True, stop=True)
                elif name == "up":
                    if n % GB <= 1:
                        pe.wait_ge(xin_ready, 2 * (n // GB) + 1 + n % GB)
                    if n == 0:
                        pe.wait_ge(UU_ready, R)
                    parts = [v[:, BC * (n % GB):BC * (n % GB) + BC] for v in img[n // GB % 2]]
                    for t in range(R):
                        ins = convolve(s[:, BC * t:BC * t + BC],
                                       [(UU[:, i, R * k - t + NS - 1, :, :], parts[j], k) for k in (-1, 0, 1) if 0 <= R * k - t + NS - 1 < SPAN
                                        for i, j in ((0, 0), (0, 1), (1, 0))])
                elif name == "down":
                    pe.wait_ge(y_ready, n + 1)
                    if n == 0:
                        pe.wait_ge(a_drained, A["dnT", 0] + 1)
                    ins = convolve(s[:, 0:BC], [(DD[:, i, R * k + t + 3, :, :], y_parts[n % 2][j][:, BC * t:BC * t + BC], k) for k in (-1, 0, 1)
                                                for t in range(R) if 0 <= R * k + t + 3 < SPAN for i, j in ((0, 0), (0, 1), (1, 0))])
                elif name == "tok":
                    pe.wait_ge(a_drained, A["down", n] + 1)
                    for k in range(HB):
                        nc.tensor.transpose(s[:, P * k:P * k + P], image_cols(n, k), ident)
                    for k in range(HB):
                        ins = nc.tensor.matmul(s[:, BC + P * k:BC + P * k + P], image_cols(n, k), cst[:, C_Q:C_Q + P], start=True, stop=True)
                elif name == "zK":
                    pe.wait_ge(z4_ready, n + 1)
                    if n == 0:
                        pe.wait_ge(masks_ready, 3)
                    ins = turn(s.bitcast(F16), lambda k: z4[:, n % 2, k, :, :], ident_h[:, :])
                elif name == "zV":
                    ins = turn(s.bitcast(F16), lambda k: zK[0:2 * C, n % 3, P * k:P * k + P], ident_h[0:2 * C, 0:2 * C], 2 * C)
                elif name == "yQ":
                    pe.wait_ge(b_drained, BU["zK", n] + 1)
                    if n == 0:
                        pe.wait_ge(a_drained, A["small", 2] + 1)
                    for i in range(2):
                        ins = nc.tensor.matmul(s[:, BANK * i:BANK * i + BANK], BB[:, :, :], zK[:, n % 3, BANK * i:BANK * i + BANK], start=True, stop=True)
                elif name == "score":
                    if e[2] == 0:
                        pe.wait_ge(a_drained, A["yQ", n] + 1)
                    for m, at in packed(e[2]):
                        for lo, hi in pieces(at, at + P * m):
                            diagonal = hi == at + P * m
                            ins = nc.tensor.matmul(s[:, lo:hi], yQ[:, n % 3, P * (m - 1):P * m], zK[:, n % 3, lo - at:hi - at],
                                                   start=True, stop=not diagonal)
                            if diagonal:
                                ins = nc.tensor.matmul(s[:, hi - P:hi], ident_b[:, :], mask_b[:, :], start=False, stop=True)
                elif name == "shift":
                    pe.wait_ge(max_ready, n + 1)
                    ins = turn(s.bitcast(F16), lambda k: M4[:, k, :, :], ident_h[:, :])
                elif name == "prob":
                    if e[2] == 0:
                        pe.wait_ge(a_drained, A["shift", n] + 1)
                    for m, at in packed(e[2]):
                        j = KT - m
                        for lo, hi in pieces(at, at + P * m):
                            diagonal = lo == at
                            ins = nc.tensor.matmul(s[:, lo:hi], zK[:, n % 3, P * j:P * j + P], yQ[:, n % 3, P * j + lo - at:P * j + hi - at],
                                                   start=True, stop=not diagonal)
                            if diagonal:
                                ins = nc.tensor.matmul(s[:, lo:lo + P], mask_b[:, :], ident_b[:, :], start=False, stop=True)
                elif name == "pv":
                    pe.wait_ge(b_drained, BU["zV", n] + 1)
                    waited = set()
                    for j in range(KT):
                        unit = next(u_ for u_ in range(NU) if KT - j in PACK[u_])
                        if unit not in waited:
                            waited.add(unit)
                            pe.wait_ge(*low_count(n, unit))
                        for i in range(2):
                            last = R * (i + 1) - 1
                            if j > last:
                                continue
                            q = max(P * j, BANK * i)
                            N = BANK * (i + 1) - q
                            o = PLACE[j] + q - P * j
                            for part in range(2):
                                ins = nc.tensor.matmul(s[0:2 * C, q:q + N], zV[:, n % 3, j, :], Pp[:, n % 2, part, o:o + N],
                                                       start=j == 0 and part == 0, stop=j == last and part == 1)
                elif name == "proj":
                    pe.wait_ge(b_drained, BU["pv", GB * n + 2 * e[2] + 1] + 1)
                    tile = by_tile(oT[:, e[2], :])
                    for k in range(KT):
                        ins = nc.tensor.matmul(s[:, P * k:P * k + 2 * C + 2], tile(k), V2[:, :], start=True, stop=True)
                elif name == "uT":
                    pe.wait_ge(u_ready, 2 * n + 2)
                    ins = turn(s, lambda k: u[:, k, :], ident)
                elif name == "logits":
                    pe.wait_ge(a_drained, A["uT", n] + 1)
                    for i in range(2):
                        ins = nc.tensor.matmul(s[0:GE, BANK * i:BANK * i + BANK], gateT[:, :, :], uT[:, BANK * i:BANK * i + BANK], start=True, stop=True)
                elif name == "wT":
                    pe.wait_ge(route_ready, n + 1)
                    ins = turn(s, by_tile(xF_all[0:GE, n, :]), ident[0:GE, 0:GE], GE)
                elif name == "pool":
                    pe.wait_ge(a_drained, A["wT", n] + 1)
                    for k in range(KT):
                        ins = nc.tensor.matmul(s[:, 0:GE], u[:, k, :], wT[:, k, :], start=k == 0, stop=k == KT - 1)
                elif name == "hidden":
                    first, last = PARTS[n]
                    if n == 0:
                        pe.wait_ge(w1_split, 2)
                    pe.wait_ge(pooled_split, 2 * (last // GB))
                    for x_ in range(E_):
                        ins = nc.tensor.matmul(s[:, B * x_ + first:B * x_ + last], w1_parts[:, x_, :], pooled[:, x_, first:last], start=True, stop=True)
                elif name == "experts":
                    first, last = PARTS[n]
                    pe.wait_ge(b_drained, BU["hidden", n] + 1)
                    sv = s[0:C, 0:B * E_].rearrange("p (b e) -> p e b", b=B)[:, :, first:last]
                    for x_ in range(E_):
                        ins = nc.tensor.matmul(sv[:, x_, :], w2_sb[:, x_, :], hid[:, x_, first:last], start=True, stop=True)
                elif name == "turned":
                    pe.wait_ge(a_drained, A["experts", n] + 1)
                    for g in range(PARTS[n][0] // GB, PARTS[n][1] // GB):
                        ins = nc.tensor.transpose(s[0:GE, C * g:C * g + C], o2[:, GB * g:GB * g + GB, :], ident[0:C, 0:C])
                elif name == "scatter":
                    pe.wait_ge(a_drained, A["turned", n // (G - 1)] + 1)
                    tile = by_tile(xF_all[0:GE, n, :])
                    for k in range(KT):
                        ins = nc.tensor.matmul(s[:, P * k:P * k + P], tile(k), obd[:, n, :, :], start=True, stop=True)
                        if k == R - 1:
                            ins.then_inc(half_filled, 1)
                else:
                    continue
                ins.then_inc(a_filled if e in A else b_filled, 1)


_INS = ['x', 'L0_conv_bias', 'L0_conv_up_filter', 'L0_conv_dn_filter', 'L1_attn_Wq', 'L1_attn_Wk', 'L1_attn_Wv',
        'L1_ffn_gate_w', 'L1_ffn_gate_b', 'L1_ffn_weight1', 'L1_ffn_weight2']
_OUTS = [((16, 32, 32, 32), 'float32')]


def kernel(**inputs):
    import numpy as _np
    import concourse.bacc as _bacc
    from concourse import mybir as _mybir
    from concourse.bass_utils import run_bass_kernel_spmd as _run

    nc = _bacc.Bacc("TRN2", target_bir_lowering=False, num_devices=1)
    arrays, args = {}, []
    for name in _INS:
        a = _np.ascontiguousarray(inputs[name])
        arrays[f"in_{name}_dram"] = a
        args.append(nc.dram_tensor(f"in_{name}_dram", a.shape, _mybir.dt.from_np(a.dtype), kind="ExternalInput").ap())
    for i, (shape, dtype) in enumerate(_OUTS):
        dt = _mybir.dt.from_np(_np.dtype(dtype))
        args.append(nc.dram_tensor(f"out_{i}_dram", shape, dt, kind="ExternalOutput").ap())
    hybrid_kernel(nc, *args)
    r = _run(nc, [arrays], core_ids=[0])
    return r.results[0]["out_0_dram"]
```
